# Optimizing a Trainium2 kernel written in Bass

```python
import numpy as np
import jax
import jax.numpy as jnp

def _softmax(x, axis=-1):
    return jax.nn.softmax(x, axis=axis)

def _gelu(x):
    return jax.nn.gelu(x, approximate=True)

def _silu(x):
    return jax.nn.silu(x)

def _sigmoid(x):
    return jax.nn.sigmoid(x)

def _layernorm(x, axis=-1, eps=1e-05):
    m = jnp.mean(x, axis=axis, keepdims=True)
    v = jnp.var(x, axis=axis, keepdims=True)
    return (x - m) / jnp.sqrt(v + eps)

def _scatter_add(tgt, idx, src, axis=0):
    return tgt.at[idx].add(src)

def _segment_sum(src, seg, n):
    return jax.ops.segment_sum(src, seg, n)
kernel_name = 'mk_seq_postln_d2_jaxref_r8_9fff14'

def setup_inputs(seed: int=0):
    np.random.seed(seed)
    _w = jnp.asarray

    def _L0_attn_setup():
        import jax, jax.numpy as jnp
        import numpy as np
        import math
        B, S, E, H = (2, 256, 128, 16)
        D = E // H
        SCALE = 1.0 / math.sqrt(D)
        key = jax.random.key(seed)
        ks = jax.random.split(key, 5)
        std = 0.02
        return {'q': jax.random.normal(ks[0], (B, S, E), dtype=jnp.float32), 'Wq': jax.random.normal(ks[1], (E, H * D), dtype=jnp.float32) * std, 'Wk': jax.random.normal(ks[2], (E, H * D), dtype=jnp.float32) * std, 'Wv': jax.random.normal(ks[3], (E, H * D), dtype=jnp.float32) * std, 'Wo': jax.random.normal(ks[4], (H * D, E), dtype=jnp.float32) * std, 'gamma': jnp.ones((H,), dtype=jnp.float32)}
    _L0_attn_in = _L0_attn_setup()

    def _L0_ffn_setup():
        import jax, jax.numpy as jnp
        import numpy as np
        H = 128
        I = 88
        E = 64
        TOP_K = 8
        NG = 8
        TOPK_GROUP = 4
        N_SHARED = 2
        ROUTED_SCALE = 2.5
        S_I = I * N_SHARED

        def _route(x, gate_w, gate_bias):
            T = x.shape[0]
            logits = x @ gate_w.T
            scores = jax.nn.sigmoid(logits)
            scores_for_choice = scores + gate_bias[None, :]
            grp = scores_for_choice.reshape(T, NG, E // NG)
            group_scores = jnp.sum(jax.lax.top_k(grp, 2)[0], axis=-1)
            _, gidx = jax.lax.top_k(group_scores, TOPK_GROUP)
            gmask = jnp.zeros((T, NG), dtype=scores.dtype).at[jnp.arange(T)[:, None], gidx].set(1.0)
            emask = jnp.repeat(gmask, E // NG, axis=1)
            masked = jnp.where(emask > 0, scores_for_choice, 0.0)
            _, topk_idx = jax.lax.top_k(masked, TOP_K)
            topk_w = jnp.take_along_axis(scores, topk_idx, axis=1)
            topk_w = topk_w / (jnp.sum(topk_w, axis=-1, keepdims=True) + 1e-20)
            topk_w = topk_w * ROUTED_SCALE
            rw = jnp.zeros((T, E), dtype=scores.dtype).at[jnp.arange(T)[:, None], topk_idx].add(topk_w)
            return rw

        def _mlp(x, gw, uw, dw):
            return jax.nn.silu(x @ gw.T) * (x @ uw.T) @ dw.T
        key = jax.random.key(seed)
        ks = jax.random.split(key, 10)
        sc = 0.02
        return {'hidden_states': jax.random.normal(ks[0], (1, 128, H), dtype=jnp.float32), 'gate_w': sc * jax.random.normal(ks[1], (E, H), dtype=jnp.float32), 'gate_bias': sc * jax.random.normal(ks[2], (E,), dtype=jnp.float32), 'Wg': sc * jax.random.normal(ks[3], (E, I, H), dtype=jnp.float32), 'Wu': sc * jax.random.normal(ks[4], (E, I, H), dtype=jnp.float32), 'Wd': sc * jax.random.normal(ks[5], (E, H, I), dtype=jnp.float32), 'Sg': sc * jax.random.normal(ks[6], (S_I, H), dtype=jnp.float32), 'Su': sc * jax.random.normal(ks[7], (S_I, H), dtype=jnp.float32), 'Sd': sc * jax.random.normal(ks[8], (H, S_I), dtype=jnp.float32)}
    _L0_ffn_in = _L0_ffn_setup()

    def _L1_attn_setup():
        import jax, jax.numpy as jnp
        import numpy as np
        import math
        B, S, D = (4, 256, 128)
        H = 16
        HD = D // H
        DL = 32
        LAMBDA_DECAY = 0.01
        key = jax.random.key(seed)
        ks = jax.random.split(key, 8)
        sc = lambda fan_in: 1.0 / math.sqrt(fan_in)
        return {'x': jax.random.normal(ks[0], (B, S, D), dtype=jnp.float32), 'W_q': jax.random.normal(ks[1], (D, D), dtype=jnp.float32) * sc(D), 'W_k': jax.random.normal(ks[2], (D, D), dtype=jnp.float32) * sc(D), 'W_v': jax.random.normal(ks[3], (D, D), dtype=jnp.float32) * sc(D), 'W_o': jax.random.normal(ks[4], (D, D), dtype=jnp.float32) * sc(D), 'W_down_kv': jax.random.normal(ks[5], (D, DL), dtype=jnp.float32) * sc(D), 'W_up_k': jax.random.normal(ks[6], (DL, D), dtype=jnp.float32) * sc(DL), 'W_up_v': jax.random.normal(ks[7], (DL, D), dtype=jnp.float32) * sc(DL)}
    _L1_attn_in = _L1_attn_setup()

    def _L1_ffn_setup():
        import jax, jax.numpy as jnp
        import numpy as np
        import math
        N_EMBD = 128
        HIDDEN = 4 * N_EMBD
        N_EXPERTS = 8
        TOP_K = 2
        B, T = (4, 256)

        def new_gelu(x):
            c = math.sqrt(2.0 / math.pi)
            return 0.5 * x * (1.0 + jnp.tanh(c * (x + 0.044715 * x * x * x)))

        def _moe_forward(x, Wfc_s, bfc_s, Wproj_s, bproj_s, Wr, Wfc, bfc, Wproj, bproj):
            Bb, Tt, C = x.shape
            xf = x.reshape(Bb * Tt, C)
            N = Bb * Tt
            shared = new_gelu(xf @ Wfc_s + bfc_s) @ Wproj_s + bproj_s
            logits = xf @ Wr
            probs = jax.nn.softmax(logits, axis=-1)
            topk_p, topk_i = jax.lax.top_k(probs, TOP_K)
            topk_p = topk_p / jnp.sum(topk_p, axis=-1, keepdims=True)
            gate = jnp.zeros((N, N_EXPERTS), dtype=xf.dtype)
            gate = gate.at[jnp.arange(N)[:, None], topk_i].add(topk_p)
            routed = jnp.zeros_like(xf)
            for e in range(N_EXPERTS):
                h = new_gelu(xf @ Wfc[e] + bfc[e]) @ Wproj[e] + bproj[e]
                routed = routed + h * gate[:, e:e + 1]
            return (shared + routed).reshape(Bb, Tt, C)
        key = jax.random.key(seed)
        ks = jax.random.split(key, 10)
        s = 0.02
        return {'x': jax.random.normal(ks[0], (B, T, N_EMBD), dtype=jnp.float32), 'Wfc_s': jax.random.normal(ks[1], (N_EMBD, HIDDEN), dtype=jnp.float32) * s, 'bfc_s': jnp.zeros((HIDDEN,), dtype=jnp.float32), 'Wproj_s': jax.random.normal(ks[2], (HIDDEN, N_EMBD), dtype=jnp.float32) * s, 'bproj_s': jnp.zeros((N_EMBD,), dtype=jnp.float32), 'Wr': jax.random.normal(ks[3], (N_EMBD, N_EXPERTS), dtype=jnp.float32) * s, 'Wfc': jax.random.normal(ks[4], (N_EXPERTS, N_EMBD, HIDDEN), dtype=jnp.float32) * s, 'bfc': jnp.zeros((N_EXPERTS, HIDDEN), dtype=jnp.float32), 'Wproj': jax.random.normal(ks[5], (N_EXPERTS, HIDDEN, N_EMBD), dtype=jnp.float32) * s, 'bproj': jnp.zeros((N_EXPERTS, N_EMBD), dtype=jnp.float32)}
    _L1_ffn_in = _L1_ffn_setup()
    _d = {'L0_attn_q': _L0_attn_in['q'], 'L0_attn_Wq': _L0_attn_in['Wq'], 'L0_attn_Wk': _L0_attn_in['Wk'], 'L0_attn_Wv': _L0_attn_in['Wv'], 'L0_attn_Wo': _L0_attn_in['Wo'], 'L0_attn_gamma': _L0_attn_in['gamma'], 'L0_ffn_gate_w': _L0_ffn_in['gate_w'], 'L0_ffn_gate_bias': _L0_ffn_in['gate_bias'], 'L0_ffn_Wg': _L0_ffn_in['Wg'], 'L0_ffn_Wu': _L0_ffn_in['Wu'], 'L0_ffn_Wd': _L0_ffn_in['Wd'], 'L0_ffn_Sg': _L0_ffn_in['Sg'], 'L0_ffn_Su': _L0_ffn_in['Su'], 'L0_ffn_Sd': _L0_ffn_in['Sd'], 'L1_attn_W_q': _L1_attn_in['W_q'], 'L1_attn_W_k': _L1_attn_in['W_k'], 'L1_attn_W_v': _L1_attn_in['W_v'], 'L1_attn_W_o': _L1_attn_in['W_o'], 'L1_attn_W_down_kv': _L1_attn_in['W_down_kv'], 'L1_attn_W_up_k': _L1_attn_in['W_up_k'], 'L1_attn_W_up_v': _L1_attn_in['W_up_v'], 'L1_ffn_Wfc_s': _L1_ffn_in['Wfc_s'], 'L1_ffn_bfc_s': _L1_ffn_in['bfc_s'], 'L1_ffn_Wproj_s': _L1_ffn_in['Wproj_s'], 'L1_ffn_bproj_s': _L1_ffn_in['bproj_s'], 'L1_ffn_Wr': _L1_ffn_in['Wr'], 'L1_ffn_Wfc': _L1_ffn_in['Wfc'], 'L1_ffn_bfc': _L1_ffn_in['bfc'], 'L1_ffn_Wproj': _L1_ffn_in['Wproj'], 'L1_ffn_bproj': _L1_ffn_in['bproj']}
    _x0 = _d['L0_attn_q']
    _d['L0_attn_q'] = jax.random.normal(jax.random.fold_in(jax.random.key(seed), 1), (2, 1024, 128), dtype=_x0.dtype)
    del _x0
    return _d

def reference(L0_attn_q, L0_attn_Wq, L0_attn_Wk, L0_attn_Wv, L0_attn_Wo, L0_attn_gamma, L0_ffn_gate_w, L0_ffn_gate_bias, L0_ffn_Wg, L0_ffn_Wu, L0_ffn_Wd, L0_ffn_Sg, L0_ffn_Su, L0_ffn_Sd, L1_attn_W_q, L1_attn_W_k, L1_attn_W_v, L1_attn_W_o, L1_attn_W_down_kv, L1_attn_W_up_k, L1_attn_W_up_v, L1_ffn_Wfc_s, L1_ffn_bfc_s, L1_ffn_Wproj_s, L1_ffn_bproj_s, L1_ffn_Wr, L1_ffn_Wfc, L1_ffn_bfc, L1_ffn_Wproj, L1_ffn_bproj):

    def _L0_attn_ref(q, Wq, Wk, Wv, Wo, gamma):
        import jax, jax.numpy as jnp
        import numpy as np
        import math
        B, S, E, H = (2, 256, 128, 16)
        D = E // H
        SCALE = 1.0 / math.sqrt(D)
        Bq, Sq, _ = q.shape
        qh = (q @ Wq).reshape(Bq, Sq, H, D).transpose(0, 2, 1, 3)
        kh = (q @ Wk).reshape(Bq, Sq, H, D).transpose(0, 2, 1, 3)
        vh = (q @ Wv).reshape(Bq, Sq, H, D).transpose(0, 2, 1, 3)
        q_norm = jnp.sum(qh * qh, axis=-1, keepdims=True)
        k_norm = jnp.sum(kh * kh, axis=-1, keepdims=True)
        qk = jnp.einsum('bhsd,bhtd->bhst', qh, kh)
        dist = jnp.maximum(q_norm - 2.0 * qk + jnp.swapaxes(k_norm, -2, -1), 0.0)
        scores = jnp.exp(-gamma[None, :, None, None] * SCALE * dist)
        mask = jnp.triu(jnp.ones((Sq, Sq), dtype=bool), k=1)
        scores = jnp.where(mask, scores, 0.0)
        out = jnp.einsum('bhst,bhtd->bhsd', scores, vh)
        out = out.transpose(0, 2, 1, 3).reshape(Bq, Sq, H * D)
        return out @ Wo

    def _L0_ffn_ref(hidden_states, gate_w, gate_bias, Wg, Wu, Wd, Sg, Su, Sd):
        import jax, jax.numpy as jnp
        import numpy as np
        H = 128
        I = 88
        E = 64
        TOP_K = 8
        NG = 8
        TOPK_GROUP = 4
        N_SHARED = 2
        ROUTED_SCALE = 2.5
        S_I = I * N_SHARED

        def _route(x, gate_w, gate_bias):
            T = x.shape[0]
            logits = x @ gate_w.T
            scores = jax.nn.sigmoid(logits)
            scores_for_choice = scores + gate_bias[None, :]
            grp = scores_for_choice.reshape(T, NG, E // NG)
            group_scores = jnp.sum(jax.lax.top_k(grp, 2)[0], axis=-1)
            _, gidx = jax.lax.top_k(group_scores, TOPK_GROUP)
            gmask = jnp.zeros((T, NG), dtype=scores.dtype).at[jnp.arange(T)[:, None], gidx].set(1.0)
            emask = jnp.repeat(gmask, E // NG, axis=1)
            masked = jnp.where(emask > 0, scores_for_choice, 0.0)
            _, topk_idx = jax.lax.top_k(masked, TOP_K)
            topk_w = jnp.take_along_axis(scores, topk_idx, axis=1)
            topk_w = topk_w / (jnp.sum(topk_w, axis=-1, keepdims=True) + 1e-20)
            topk_w = topk_w * ROUTED_SCALE
            rw = jnp.zeros((T, E), dtype=scores.dtype).at[jnp.arange(T)[:, None], topk_idx].add(topk_w)
            return rw

        def _mlp(x, gw, uw, dw):
            return jax.nn.silu(x @ gw.T) * (x @ uw.T) @ dw.T
        B, S, _ = hidden_states.shape
        x = hidden_states.reshape(B * S, H)
        rw = _route(x, gate_w, gate_bias)
        expert_out = jax.vmap(lambda gw_, uw_, dw_: _mlp(x, gw_, uw_, dw_))(Wg, Wu, Wd)
        routed = jnp.einsum('eth,te->th', expert_out, rw)
        shared = _mlp(x, Sg, Su, Sd)
        out = (routed + shared).reshape(B, S, H)
        return out

    def _L1_attn_ref(x, W_q, W_k, W_v, W_o, W_down_kv, W_up_k, W_up_v):
        import jax, jax.numpy as jnp
        import numpy as np
        import math
        B, S, D = (4, 256, 128)
        H = 16
        HD = D // H
        DL = 32
        LAMBDA_DECAY = 0.01
        b, s, d = x.shape
        q = x @ W_q
        k = x @ W_k
        v = x @ W_v
        latent_kv = (k + v) @ W_down_kv
        k_rec = (latent_kv @ W_up_k).reshape(b, s, H, HD).transpose(0, 2, 1, 3)
        v_rec = (latent_kv @ W_up_v).reshape(b, s, H, HD).transpose(0, 2, 1, 3)
        qh = q.reshape(b, s, H, HD).transpose(0, 2, 1, 3)
        scores = jnp.einsum('bhqd,bhkd->bhqk', qh, k_rec) / math.sqrt(d)
        t = jnp.arange(s, dtype=jnp.float32)
        decay = jnp.exp(-LAMBDA_DECAY * jnp.abs(t[:, None] - t[None, :]))
        scores = scores * decay[None, None, :, :]
        attn = jax.nn.softmax(scores, axis=-1)
        out = jnp.einsum('bhqk,bhkd->bhqd', attn, v_rec)
        out = out.transpose(0, 2, 1, 3).reshape(b, s, d)
        return out @ W_o

    def _L1_ffn_ref(x, Wfc_s, bfc_s, Wproj_s, bproj_s, Wr, Wfc, bfc, Wproj, bproj):
        import jax, jax.numpy as jnp
        import numpy as np
        import math
        N_EMBD = 128
        HIDDEN = 4 * N_EMBD
        N_EXPERTS = 8
        TOP_K = 2
        B, T = (4, 256)

        def new_gelu(x):
            c = math.sqrt(2.0 / math.pi)
            return 0.5 * x * (1.0 + jnp.tanh(c * (x + 0.044715 * x * x * x)))

        def _moe_forward(x, Wfc_s, bfc_s, Wproj_s, bproj_s, Wr, Wfc, bfc, Wproj, bproj):
            Bb, Tt, C = x.shape
            xf = x.reshape(Bb * Tt, C)
            N = Bb * Tt
            shared = new_gelu(xf @ Wfc_s + bfc_s) @ Wproj_s + bproj_s
            logits = xf @ Wr
            probs = jax.nn.softmax(logits, axis=-1)
            topk_p, topk_i = jax.lax.top_k(probs, TOP_K)
            topk_p = topk_p / jnp.sum(topk_p, axis=-1, keepdims=True)
            gate = jnp.zeros((N, N_EXPERTS), dtype=xf.dtype)
            gate = gate.at[jnp.arange(N)[:, None], topk_i].add(topk_p)
            routed = jnp.zeros_like(xf)
            for e in range(N_EXPERTS):
                h = new_gelu(xf @ Wfc[e] + bfc[e]) @ Wproj[e] + bproj[e]
                routed = routed + h * gate[:, e:e + 1]
            return (shared + routed).reshape(Bb, Tt, C)
        return _moe_forward(x, Wfc_s, bfc_s, Wproj_s, bproj_s, Wr, Wfc, bfc, Wproj, bproj)
    x = L0_attn_q
    x = _layernorm(x + _L0_attn_ref(x, L0_attn_Wq, L0_attn_Wk, L0_attn_Wv, L0_attn_Wo, L0_attn_gamma), axis=-1)
    x = _layernorm(x + _L0_ffn_ref(x, L0_ffn_gate_w, L0_ffn_gate_bias, L0_ffn_Wg, L0_ffn_Wu, L0_ffn_Wd, L0_ffn_Sg, L0_ffn_Su, L0_ffn_Sd), axis=-1)
    x = _layernorm(x + _L1_attn_ref(x, L1_attn_W_q, L1_attn_W_k, L1_attn_W_v, L1_attn_W_o, L1_attn_W_down_kv, L1_attn_W_up_k, L1_attn_W_up_v), axis=-1)
    x = _layernorm(x + _L1_ffn_ref(x, L1_ffn_Wfc_s, L1_ffn_bfc_s, L1_ffn_Wproj_s, L1_ffn_bproj_s, L1_ffn_Wr, L1_ffn_Wfc, L1_ffn_bfc, L1_ffn_Wproj, L1_ffn_bproj), axis=-1)
    return x

_drawn_inputs = setup_inputs


def setup_inputs(seed=0):
    import zlib

    import numpy as np

    out = dict(_drawn_inputs(seed))
    spreads = {'L0_attn_gamma': (1.0, 0.2),
     'L1_ffn_bfc_s': (0.0, 0.313),
     'L1_ffn_bproj_s': (0.0, 0.1),
     'L1_ffn_bfc': (0.0, 0.476),
     'L1_ffn_bproj': (0.0, 0.1)}
    factors = {'L0_ffn_gate_w': 8.0,
     'L0_ffn_gate_bias': 8.0,
     'L0_ffn_Wg': 8.0,
     'L0_ffn_Wu': 8.0,
     'L0_ffn_Wd': 8.0,
     'L0_ffn_Sg': 6.83,
     'L0_ffn_Su': 6.636,
     'L0_ffn_Sd': 6.44,
     'L1_attn_W_q': 3.129,
     'L1_attn_W_up_k': 3.244}
    for name, (base, spread) in spreads.items():
        noise = np.random.default_rng([zlib.crc32(name.encode()), seed]).standard_normal(out[name].shape)
        drawn = base * np.exp(spread * noise) if base else spread * noise
        out[name] = jnp.asarray(drawn.astype(out[name].dtype))
    for name, factor in factors.items():
        out[name] = (out[name] * factor).astype(out[name].dtype)
    return out
```

```python
from contextlib import ExitStack

import numpy as np

import concourse.bass as bass
from concourse import mybir

F32 = mybir.dt.float32
F32R = mybir.dt.float32r
BF16 = mybir.dt.bfloat16
ALU = mybir.AluOpType
ACT = mybir.ActivationFunctionType
AX = mybir.AxisListType

B, S, E = 2, 1024, 128
TOK = B * S
P = 128
H, HD = 16, 8
HQ = 4
NQUAD = H // HQ
NIT = B * NQUAD
HP = P // HQ
KB = S // P
GW = 512
NG = TOK // GW
NPART = 3
PAIRS = NPART * NPART * HD
ONES_ROW = 96
EPS = 1e-5
BF16_ONES = float(np.array([0x3F803F80], np.uint32).view(np.float32)[0])

NE0, I0 = 64, 88
NGRP, GSZ, TOPG, TOP0 = 8, 8, 4, 8
ROUTED_SCALE = 2.5
CH0 = NE0 * I0 // P
SHI = 2 * I0
CHS = -(-SHI // P)
DL = 32
DECAY = 0.01
NE1, HID = 8, 512
CH1 = HID // P




class Sems:

    def __init__(self, nc, ctx):
        self.nc, self.ctx = nc, ctx

    def __call__(self, name):
        return self.ctx.enter_context(self.nc.semaphore(name))


def wait(eng, sem, value):
    if not isinstance(value, int) or value > 0:
        eng.wait_ge(sem, value)


def sbuf(nc, ctx):
    return lambda name, shape, dt: ctx.enter_context(nc.sbuf_tensor(name, shape, dt))


def psum(nc, ctx):
    return lambda name, width=GW: ctx.enter_context(nc.psum_tensor(name, [P, width], F32))


def split3(dve, nc, done, n, parts, rest, src, ready=None):
    p1, p2, p3 = parts
    nc.vector.tensor_copy(p1, src).then_inc(done, 1)
    dve.wait_ge(done, n + 1)
    nc.vector.tensor_tensor(rest, src, p1, ALU.subtract).then_inc(done, 1)
    dve.wait_ge(done, n + 2)
    nc.vector.tensor_copy(p2, rest).then_inc(done, 1)
    dve.wait_ge(done, n + 3)
    nc.vector.tensor_tensor(p3, rest, p2, ALU.subtract).then_inc(done, 1)


def project_l0(nc, X, wq, wk, headsel, QS, KS, QN, KN):
    with ExitStack() as ctx:
        sb, pb, sem = sbuf(nc, ctx), psum(nc, ctx), Sems(nc, ctx)
        Wq, Wk = sb("p0_Wq", [P, P], F32), sb("p0_Wk", [P, P], F32)
        Hs = sb("p0_Hs", [P, H], F32)
        sq, sk = sb("p0_sq", [P, GW], F32), sb("p0_sk", [P, GW], F32)
        k2 = sb("p0_k2", [P, GW], F32)
        rest = sb("p0_rest", [P, 4, GW], F32)
        qp, kp = sb("p0_qp", [P, NPART, GW], BF16), sb("p0_kp", [P, NPART, GW], BF16)
        qn, kn = sb("p0_qn", [H, NPART, GW], BF16), sb("p0_kn", [H, NPART, GW], BF16)
        psQ, psK, psQN, psKN = pb("p0_psQ"), pb("p0_psK"), pb("p0_psQN"), pb("p0_psKN")
        loaded, proj_ready, sq_ready, norm_ready = sem("loaded"), sem("proj_ready"), sem("sq_ready"), sem("norm_ready")
        split_done, stored = sem("split_done"), sem("stored")
        STEPS = 16
        STORES = 3 + 5 + 3 + 3
        with nc.Block() as block:
            @block.sync
            def _(sp):
                sp.dma_start(Wq[:], wq).then_inc(loaded, 16)
                sp.dma_start(Wk[:], wk).then_inc(loaded, 16)
                sp.dma_start(Hs[:], headsel).then_inc(loaded, 16)
                def group(g):
                    tok = bass.ds(g * GW, GW)
                    wait(sp, split_done, g * STEPS + 8)
                    for i in range(NPART):
                        sp.dma_start(QS[:, i, :, tok], qp[:, i, :]).then_inc(stored, 16)
                    for i in range(NPART + 2):
                        sp.dma_start(KS[:, i, :, tok], kp[:, i % NPART, :]).then_inc(stored, 16)
                    wait(sp, split_done, (g + 1) * STEPS)
                    sp.dma_start(QN[:, :, tok], qn[:]).then_inc(stored, 16)
                    sp.dma_start(KN[:, :, tok], kn[:]).then_inc(stored, 16)
                group(0)
                with sp.Fori(1, NG) as g:
                    group(g)
                sp.wait_ge(stored, NG * (STORES - 4) * 16)

            @block.tensor
            def _(pe):
                pe.wait_ge(loaded, 48)
                def group(g):
                    xg = X[:, bass.ds(g * GW, GW)]
                    wait(pe, split_done, g * STEPS)
                    nc.tensor.matmul(psQ[:], Wq[:], xg, start=True, stop=True).then_inc(proj_ready, 1)
                    nc.tensor.matmul(psK[:], Wk[:], xg, start=True, stop=True).then_inc(proj_ready, 1)
                    wait(pe, sq_ready, g * 3 + 1)
                    nc.tensor.matmul(psQN[0:H, :], Hs[:], sq[:], start=True, stop=True).then_inc(norm_ready, 1)
                    wait(pe, sq_ready, g * 3 + 2)
                    nc.tensor.matmul(psKN[0:H, :], Hs[:], sk[:], start=True, stop=True).then_inc(norm_ready, 1)
                group(0)
                with pe.Fori(1, NG) as g:
                    group(g)

            @block.scalar
            def _(act):
                def group(g):
                    wait(act, proj_ready, g * 2 + 1)
                    wait(act, norm_ready, g * 2)
                    nc.scalar.activation(sq[:], psQ[:], ACT.Square).then_inc(sq_ready, 1)
                    wait(act, proj_ready, g * 2 + 2)
                    nc.scalar.activation(sk[:], psK[:], ACT.Square).then_inc(sq_ready, 1)
                    wait(act, split_done, g * STEPS)
                    nc.scalar.activation(k2[:], psK[:], ACT.Copy, scale=-2.0).then_inc(sq_ready, 1)
                group(0)
                with act.Fori(1, NG) as g:
                    group(g)

            @block.vector
            def _(dve):
                def group(g):
                    n = g * STEPS
                    wait(dve, stored, g * ((STORES - 4) * 16))
                    wait(dve, sq_ready, g * 3 + 3)
                    split3(dve, nc, split_done, n, [qp[:, i, :] for i in range(3)], rest[:, 0, :], psQ[:])
                    split3(dve, nc, split_done, n + 4, [kp[:, i, :] for i in range(3)], rest[:, 1, :], k2[:])
                    wait(dve, norm_ready, g * 2 + 2)
                    split3(dve, nc, split_done, n + 8, [qn[:, i, :] for i in range(3)], rest[0:H, 2, :], psQN[0:H, :])
                    split3(dve, nc, split_done, n + 12, [kn[:, i, :] for i in range(3)], rest[0:H, 3, :], psKN[0:H, :])
                group(0)
                with dve.Fori(1, NG) as g:
                    group(g)


TILES0 = [[(7, 0, 1024)], [(6, 0, 896), (0, 896, 128)], [(5, 0, 768), (1, 768, 256)],
          [(4, 0, 640), (2, 640, 384)], [(3, 0, 512)]]
WIDTH0 = [sum(r[2] for r in t) for t in TILES0]


def pieces(a, b, cut=GW):
    while a < b:
        e = min(b, (a // cut + 1) * cut)
        yield a, e
        a = e


def attention_l0(nc, x_dram, wv, gamma, QS, KS, QN, KN, OALL):
    NT = len(TILES0)
    RING, LAG = 3, 2
    STEPS = 1 + NT * HQ
    LOADS = (3 + 3 + 2 + 2) * 16
    assert STEPS % RING == 0
    with ExitStack() as ctx:
        sb, pb, sem = sbuf(nc, ctx), psum(nc, ctx), Sems(nc, ctx)
        QP = [sb(f"a0_QP{s}", [P, HQ, S], BF16) for s in range(2)]
        KP = [sb(f"a0_KP{s}", [P, HQ, S], BF16) for s in range(2)]
        XB = [sb(f"a0_XB{s}", [P, S], F32) for s in range(2)]
        WV = [sb(f"a0_WV{s}", [P, P], F32) for s in range(2)]
        V = [sb(f"a0_V{s}", [P, S], F32) for s in range(2)]
        PR = [sb(f"a0_PR{T}", [P, HQ, S], F32) for T in range(NT)]
        gam, ng, lo, hi = (sb(f"a0_{n}", [P, H], F32) for n in ("gam", "ng", "lo", "hi"))
        ring = [pb(f"a0_ring{r}", S) for r in range(RING)]
        OUT = pb("a0_OUT", S)
        pack_loaded = [sem(f"pack_loaded{s}") for s in range(2)]
        slot_set = [sem(f"slot_set{s}") for s in range(2)]
        gamma_loaded, gamma_ready = sem("gamma_loaded"), sem("gamma_ready")
        ring_filled, ring_read, clamped, masked, pv_done, out_read = (
            sem(n) for n in ("ring_filled", "ring_read", "clamped", "masked", "pv_done", "out_read"))


        def set_slot(eng, nc_eng, s):
            for n, (rows, value) in enumerate(((QP[s][64:96], 0.0), (QP[s][96:P], BF16_ONES),
                                               (KP[s][64:96], BF16_ONES), (KP[s][96:P], 0.0))):
                if n:
                    eng.wait_ge(slot_set[s], n)
                nc_eng.memset(rows.bitcast(F32), value).then_inc(slot_set[s], 1)
            eng.wait_ge(slot_set[s], 4)

        with nc.Block() as block:
            @block.sync
            def _(sp):
                sp.dma_start(gam[:], gamma.partition_broadcast(P)).then_inc(gamma_loaded, 16)

                def load(b, q, s):
                    tok, heads = bass.ds(b * S, S), bass.ds(q * HQ, HQ)
                    got = pack_loaded[s]
                    for r in range(NPART):
                        rows = slice(r * 24, r * 24 + 24)
                        sp.dma_start(QP[s][rows], QS[heads, :, :, tok].rearrange("h i d t -> (i d) h t")).then_inc(got, 16)
                        sp.dma_start(KP[s][rows], KS[heads, r:r + 3, :, tok].rearrange("h i d t -> (i d) h t")).then_inc(got, 16)
                    sp.dma_start(QP[s][PAIRS:PAIRS + 3], QN[heads, :, tok].rearrange("h i t -> i h t")).then_inc(got, 16)
                    sp.dma_start(KP[s][ONES_ROW:ONES_ROW + 3], KN[heads, :, tok].rearrange("h i t -> i h t")).then_inc(got, 16)
                    sp.dma_start(XB[s][:], x_dram[:, tok]).then_inc(got, 16)
                    sp.dma_start(WV[s][:], wv[bass.ds(q, 1)].rearrange("a e n -> (a e) n")).then_inc(got, 16)

                for s in range(2):
                    sp.wait_ge(slot_set[s], 4)
                    load(0, s, s)
                with sp.Fori(1, NIT // 2) as k:
                    for s in range(2):
                        sp.wait_ge(ring_read, (k * 2 + (s - 1)) * STEPS)
                        sp.nop(nofuse=True)
                        load(k // 2, (k % 2) * 2 + s, s)

            @block.gpsimd
            def _(pool):
                set_slot(pool, nc.gpsimd, 1)

                def mask(it, T, s):
                    for j in range(HQ):
                        pool.wait_ge(clamped, it * (NT * HQ) + (T * HQ + j + 1))
                        pool.nop(nofuse=True)
                        for kb, c0, n in TILES0[T]:
                            d = PR[T][:, j, c0 + n - P:c0 + n]
                            last = nc.gpsimd.affine_select(out=d, in_=d, compare_op=ALU.is_gt, fill=0.0, base=0,
                                                           pattern=[[-1, P]], channel_multiplier=1)
                        last.then_inc(masked, 1)

                with pool.Fori(0, NIT // 2) as k:
                    for s in range(2):
                        for T in range(NT):
                            mask(k * 2 + s, T, s)

            @block.tensor
            def _(pe):
                def values(it, k, s):
                    pe.wait_ge(pack_loaded[s], k * LOADS + LOADS)
                    if not isinstance(it, int) or it > 0:
                        pe.wait_ge(ring_read, it * STEPS - RING + 1)
                    for kb in range(KB):
                        last = nc.tensor.matmul(ring[0][:, kb * P:(kb + 1) * P], XB[s][:, kb * P:(kb + 1) * P],
                                                WV[s][:], start=True, stop=True)
                    last.then_inc(ring_filled, 1)

                def scores(it, T, j, s):
                    n = 1 + T * HQ + j
                    if not isinstance(it, int) or it > 0 or n >= RING:
                        pe.wait_ge(ring_read, it * STEPS + (n - RING + 1))
                    for kb, c0, w in TILES0[T]:
                        for a, b in pieces(c0, c0 + w):
                            last = nc.tensor.matmul(ring[n % RING][:, a:b], KP[s][:, j, kb * P:(kb + 1) * P],
                                                    QP[s][:, j, a - c0:b - c0], start=True, stop=True)
                    last.then_inc(ring_filled, 1)

                def weigh(it, T, s, quarter):
                    if quarter == 0:
                        pe.wait_ge(masked, it * (NT * HQ) + (T + 1) * HQ)
                        if T == 0 and (not isinstance(it, int) or it > 0):
                            pe.wait_ge(out_read, it)
                    done = 0
                    for kb, c0, w in TILES0[T]:
                        for a, b in pieces(0, w, GW // 2):
                            at, done = done, done + b - a
                            if at // (GW // 2) != quarter:
                                continue
                            for j in range(HQ):
                                rows = slice(j * HP, (j + 1) * HP)
                                last = nc.tensor.matmul(OUT[rows, a:b], V[s][:, kb * P + j * HP:kb * P + (j + 1) * HP],
                                                        PR[T][:, j, c0 + a:c0 + b], start=(T == 0 and a % GW == 0),
                                                        stop=(T == NT - 1), skip_group_check=True)
                    if quarter == (WIDTH0[T] - 1) // (GW // 2):
                        last.then_inc(pv_done, 1)

                def pair(it, k, s, last_pair):
                    for T in range(NT):
                        ahead = T + LAG < NT or not last_pair
                        if T + LAG == NT and ahead:
                            values(it + 1, k + s, 1 - s)
                        for j in range(HQ):
                            if T + LAG < NT:
                                scores(it, T + LAG, j, s)
                            elif ahead:
                                scores(it + 1, T + LAG - NT, j, 1 - s)
                            for quarter in {0: (), 1: (), 2: (0, 1), 3: (2, 3)}[j] if T == 0 else (j,):
                                if quarter <= (WIDTH0[T] - 1) // (GW // 2):
                                    weigh(it, T, s, quarter)

                values(0, 0, 0)
                for T in range(LAG):
                    for j in range(HQ):
                        scores(0, T, j, 0)
                pair(0, 0, 0, False)
                pair(1, 0, 1, False)
                with pe.Fori(1, NIT // 2 - 1) as k:
                    for s in range(2):
                        pair(k * 2 + s, k, s, False)
                pair(NIT - 2, NIT // 2 - 1, 0, False)
                pair(NIT - 1, NIT // 2 - 1, 1, True)

            @block.scalar
            def _(act):
                act.wait_ge(gamma_ready, 3)

                def pair(it, b_quad, s, first):
                    act.wait_ge(ring_filled, it * STEPS + 1)
                    if not first:
                        act.wait_ge(pv_done, it * NT - NT)
                    nc.scalar.activation(V[s][:], ring[0][:], ACT.Copy).then_inc(ring_read, 1)
                    for T in range(NT):
                        for j in range(HQ):
                            n = 1 + T * HQ + j
                            act.wait_ge(ring_filled, it * STEPS + (n + 1))
                            if j == 0 and not first:
                                act.wait_ge(pv_done, it * NT + (T + 1 - NT))
                            act.nop(nofuse=True)
                            head = bass.ds(b_quad * HQ + j, 1)
                            nc.scalar.activation(PR[T][:, j, 0:WIDTH0[T]], ring[n % RING][:, 0:WIDTH0[T]],
                                                 ACT.Exp, scale=ng[:, head]).then_inc(ring_read, 1)

                pair(0, 0, 0, True)
                pair(1, 1, 1, False)
                with act.Fori(1, NIT // 2) as k:
                    for s in range(2):
                        pair(k * 2 + s, (k % 2) * 2 + s, s, False)

            @block.vector
            def _(dve):
                set_slot(dve, nc.vector, 0)
                dve.wait_ge(gamma_loaded, 16)
                nc.vector.tensor_scalar(ng[:], gam[:], -1.0 / float(np.sqrt(HD)), None, ALU.mult).then_inc(gamma_ready, 1)
                nc.vector.tensor_scalar(lo[:], gam[:], 0.0, None, ALU.is_lt).then_inc(gamma_ready, 1)
                dve.wait_ge(gamma_ready, 2)
                nc.vector.tensor_scalar(hi[:], lo[:], 3.0e38, 1.0, ALU.mult, ALU.add).then_inc(gamma_ready, 1)
                dve.wait_ge(gamma_ready, 3)

                def clamp(it, T, s, b_quad):
                    for j in range(HQ):
                        dve.wait_ge(ring_read, it * STEPS + (2 + T * HQ + j))
                        p = PR[T][:, j, 0:WIDTH0[T]]
                        head = bass.ds(b_quad * HQ + j, 1)
                        nc.vector.tensor_scalar(p, p, lo[:, head], hi[:, head], ALU.max, ALU.min).then_inc(clamped, 1)

                def copy_out(it):
                    dve.wait_ge(pv_done, it * NT + NT)
                    o = OALL[:, bass.ds(it, 1), :] if not isinstance(it, int) else OALL[:, it, :]
                    nc.vector.tensor_copy(o, OUT[:]).then_inc(out_read, 1)

                def pair(it, b_quad, s, first):
                    for T in range(NT):
                        clamp(it, T, s, b_quad)
                        if T == 1 and not first:
                            copy_out(it - 1)

                pair(0, 0, 0, True)
                pair(1, 1, 1, False)
                with dve.Fori(1, NIT // 2) as k:
                    for s in range(2):
                        pair(k * 2 + s, (k % 2) * 2 + s, s, False)
                copy_out(NIT - 1)


def add_and_norm(nc, name, X, Y, consts, terms=None, loads=()):
    mean_of = consts["mean_of"]
    with ExitStack() as ctx:
        sb, pb, sem = sbuf(nc, ctx), psum(nc, ctx), Sems(nc, ctx)
        C = [sb(f"{name}_C{g}", [P, GW], F32) for g in range(NG)]
        Q = [sb(f"{name}_Q{g}", [P, GW], F32) for g in range(NG)]
        D = [sb(f"{name}_D{g}", [P, GW], F32) for g in range(NG)]
        eps = sb(f"{name}_eps", [P, 1], F32)
        first, var = [pb(f"{name}_mean{g}") for g in range(NG)], [pb(f"{name}_var{g}") for g in range(NG)]
        loaded, delta, y_ready, mean, centred, squared, variance, dev, inv, done, eps_set = (
            sem(f"{name}_{n}") for n in ("loaded", "delta", "y_ready", "mean", "centred", "squared", "variance",
                                     "dev", "inv", "done", "eps_set"))

        def grp(t, g):
            return t[:, g * GW:(g + 1) * GW]

        with nc.Block() as block:
            if loads:
                @block.sync
                def _(sp):
                    for tile, src in loads:
                        sp.dma_start(tile, src).then_inc(loaded, 16)

            @block.tensor
            def _(pe):
                if terms:
                    pe.wait_ge(loaded, 16 * len(loads))
                    for g in range(NG):
                        pairs = terms(g)
                        for n, (a, b) in enumerate(pairs):
                            last = nc.tensor.matmul(first[g][:], a, b, start=(n == 0), stop=(n == len(pairs) - 1))
                        last.then_inc(delta, 1)
                for g in range(NG):
                    if terms:
                        pe.wait_ge(y_ready, g + 1)
                    nc.tensor.matmul(first[g][:], mean_of[:], grp(Y, g), start=True, stop=True).then_inc(mean, 1)
                for g in range(NG):
                    pe.wait_ge(squared, g + 1)
                    nc.tensor.matmul(var[g][:], mean_of[:], Q[g][:], start=True, stop=True).then_inc(variance, 1)

            @block.vector
            def _(dve):
                nc.vector.memset(eps[:], EPS).then_inc(eps_set, 1)
                if terms:
                    for g in range(NG):
                        dve.wait_ge(delta, g + 1)
                        nc.vector.tensor_tensor(grp(Y, g), grp(X, g), first[g][:], ALU.add).then_inc(y_ready, 1)
                    dve.wait_ge(y_ready, NG)
                for g in range(NG):
                    dve.wait_ge(mean, g + 1)
                    nc.vector.tensor_tensor(C[g][:], grp(Y, g), first[g][:], ALU.subtract).then_inc(centred, 1)
                for g in range(NG):
                    dve.wait_ge(dev, g + 1)
                    nc.vector.reciprocal(Q[g][:], D[g][:]).then_inc(inv, 1)
                    dve.wait_ge(inv, g + 1)
                    nc.vector.tensor_tensor(grp(X, g), C[g][:], Q[g][:], ALU.mult).then_inc(done, 1)
                dve.wait_ge(done, NG)

            @block.scalar
            def _(act):
                act.wait_ge(eps_set, 1)
                for g in range(NG):
                    act.wait_ge(centred, g + 1)
                    nc.scalar.activation(Q[g][:], C[g][:], ACT.Square).then_inc(squared, 1)
                for g in range(NG):
                    act.wait_ge(variance, g + 1)
                    nc.scalar.activation(D[g][:], var[g][:], ACT.Sqrt, bias=eps[:]).then_inc(dev, 1)


NT_TOK = TOK // P




def route_l0(nc, X, gate_w, gate_bias, earlier, consts, GT):
    with ExitStack() as ctx:
        sb, pb, sem = sbuf(nc, ctx), psum(nc, ctx), Sems(nc, ctx)
        W = sb("r0_W", [P, NE0], F32)
        bias = sb("r0_bias", [P, NE0], F32)
        tri = sb("r0_tri", [P, NGRP, NGRP], F32)
        sc = sb("r0_scores", [P, NT_TOK, NE0], F32)
        ch = sb("r0_choice", [P, NT_TOK, NE0], F32)
        t1 = sb("r0_t1", [P, NT_TOK, NE0], F32)
        t2 = sb("r0_t2", [P, NT_TOK, NE0], F32)
        m1, m2, cnt = (sb(f"r0_{n}", [P, NT_TOK * NGRP], F32) for n in ("m1", "m2", "cnt"))
        top = sb("r0_top", [P, NT_TOK, 8], F32)
        den = sb("r0_den", [P, NT_TOK], F32)
        rw = sb("r0_rw", [P, NT_TOK, 2, NE0], F32)
        psL = pb("r0_psL", NT_TOK * NE0)
        psT = [pb(f"r0_psT{g}") for g in range(NG)]
        loaded, logits, scored, step, turned, copied = (
            sem(f"r0_{n}") for n in ("loaded", "logits", "scored", "step", "turned", "copied"))
        with nc.Block() as block:
            @block.sync
            def _(sp):
                sp.dma_start(W[:], gate_w).then_inc(loaded, 16)
                sp.dma_start(bias[:], gate_bias.partition_broadcast(P)).then_inc(loaded, 16)
                sp.dma_start(tri[:], earlier.partition_broadcast(P)).then_inc(loaded, 16)

            @block.tensor
            def _(pe):
                pe.wait_ge(loaded, 48)
                for t in range(NT_TOK):
                    last = nc.tensor.matmul(psL[:, t * NE0:(t + 1) * NE0], X[:, t * P:(t + 1) * P], W[:],
                                            start=True, stop=True)
                last.then_inc(logits, 1)
                pe.wait_ge(copied, 2)
                for t in range(NT_TOK):
                    last = nc.tensor.transpose(psT[t // 4][:, (t % 4) * P:(t % 4 + 1) * P],
                                               rw[:, t].rearrange("p a e -> p (a e)"), consts["ident"][:])
                    if t % 4 == 3:
                        last.then_inc(turned, 1)

            @block.scalar
            def _(act):
                act.wait_ge(logits, 1)
                nc.scalar.activation(sc[:].rearrange("p t e -> p (t e)"), psL[:], ACT.Sigmoid).then_inc(scored, 1)

            @block.vector
            def _(dve):
                n = [0]

                def link(ins):
                    n[0] += 1
                    ins.then_inc(step, 1)
                    dve.wait_ge(step, n[0])

                v = nc.vector
                byg = lambda t: t[:].rearrange("p t (g e) -> p (t g) e", g=NGRP)
                wide = lambda t, k: t.unsqueeze(2).to_broadcast([P, NT_TOK * NGRP, k])
                dve.wait_ge(loaded, 48)
                dve.wait_ge(scored, 1)
                link(v.tensor_tensor(ch[:], sc[:], bias[:].unsqueeze(1).to_broadcast([P, NT_TOK, NE0]), ALU.add))
                link(v.tensor_reduce(m1[:], byg(ch), AX.X, ALU.max))
                link(v.tensor_tensor(byg(t1), byg(ch), wide(m1[:], GSZ), ALU.is_equal))
                link(v.scalar_tensor_tensor(t2[:], t1[:], -1e30, ch[:], ALU.mult, ALU.add))
                link(v.tensor_reduce(m2[:], byg(t2), AX.X, ALU.max))
                link(v.tensor_reduce(cnt[:], byg(t1), AX.X, ALU.add))
                link(v.tensor_scalar(cnt[:], cnt[:], 2.0, -1e30, ALU.is_lt, ALU.mult))
                link(v.tensor_tensor(cnt[:], cnt[:], m1[:], ALU.add))
                link(v.tensor_tensor(m2[:], m2[:], cnt[:], ALU.max))
                link(v.tensor_tensor(m1[:], m1[:], m2[:], ALU.add))
                gs = m1[:].rearrange("p (t g) -> p t g", g=NGRP)
                other = gs.unsqueeze(2).to_broadcast([P, NT_TOK, NGRP, NGRP])
                own = gs.unsqueeze(3).to_broadcast([P, NT_TOK, NGRP, NGRP])
                pair = lambda t: t[:].rearrange("p t (i j) -> p t i j", i=NGRP)
                link(v.tensor_tensor(pair(t1), other, own, ALU.is_gt))
                link(v.tensor_tensor(pair(t2), other, own, ALU.is_equal))
                link(v.tensor_tensor(t2[:], t2[:], tri[:].rearrange("p i j -> p (i j)").unsqueeze(1)
                                     .to_broadcast([P, NT_TOK, NE0]), ALU.mult))
                link(v.tensor_tensor(t1[:], t1[:], t2[:], ALU.add))
                link(v.tensor_reduce(cnt[:], byg(t1), AX.X, ALU.add))
                link(v.tensor_scalar(cnt[:], cnt[:], float(TOPG), None, ALU.is_lt))
                link(v.tensor_tensor(byg(t1), byg(ch), wide(cnt[:], GSZ), ALU.mult))
                for t in range(NT_TOK):
                    link(v.max(top[:, t], t1[:, t]))
                    link(v.match_replace(t2[:, t], top[:, t], t1[:, t], 1e30))
                link(v.tensor_scalar(t2[:], t2[:], 1e29, None, ALU.is_ge))
                link(v.tensor_tensor(t1[:], t2[:], sc[:], ALU.mult))
                link(v.tensor_reduce(den[:], t1[:], AX.X, ALU.add))
                link(v.tensor_scalar(den[:], den[:], 1e-20, None, ALU.add))
                link(v.reciprocal(den[:], den[:]))
                link(v.tensor_scalar(den[:], den[:], ROUTED_SCALE, None, ALU.mult))
                for a in range(2):
                    v.tensor_tensor(rw[:, :, a, :], t1[:], den[:].unsqueeze(2).to_broadcast([P, NT_TOK, NE0]),
                                    ALU.mult).then_inc(copied, 1)
                for g in range(NG):
                    dve.wait_ge(turned, g + 1)
                    cols = slice(g * GW, (g + 1) * GW)
                    link(v.tensor_copy(GT[:, cols], psT[g][:]))
                    link(v.tensor_tensor(GT[NE0:P, cols], psT[g][NE0:P, :], GT[NE0:P, cols].bitcast(F32), ALU.subtract))


def experts_l0(nc, X, Y, GT, w_chunks, sel_chunks):
    with ExitStack() as ctx:
        sb, pb, sem = sbuf(nc, ctx), psum(nc, ctx), Sems(nc, ctx)
        XH, XL = sb("e0_XH", [P, TOK], F32R), sb("e0_XL", [P, TOK], F32R)
        RAW = [sb(f"e0_RAW{s}", [P, 3, P], F32) for s in range(2)]
        WH = [sb(f"e0_WH{s}", [P, 2, P], F32R) for s in range(2)]
        WL = [sb(f"e0_WL{s}", [P, 2, P], F32R) for s in range(2)]
        SELF = [sb(f"e0_SELF{s}", [P, P], F32) for s in range(2)]
        SEL = [sb(f"e0_SEL{s}", [P, P], F32R) for s in range(2)]
        SG = [sb(f"e0_SG{s}", [P, GW], F32) for s in range(2)]
        T = [sb(f"e0_T{s}", [P, GW], F32) for s in range(2)]
        HT = [sb(f"e0_H{s}", [P, GW], F32) for s in range(2)]
        acc = [pb(f"e0_acc{g}") for g in range(NG)]
        psG = [pb(f"e0_psG{s}") for s in range(2)]
        psU, psR = pb("e0_psU"), pb("e0_psR")
        x_split = sem("x_split")
        w_loaded = [sem(f"w_loaded{s}") for s in range(2)]
        w_split = [sem(f"w_split{s}") for s in range(2)]
        gate_ready, up_ready, weight_ready, silu_done, mul_done, h_ready, down_done, y_done = (
            sem(n) for n in ("gate_ready", "up_ready", "weight_ready", "silu_done", "mul_done", "h_ready",
                             "down_done", "y_done"))
        NSH = CHS * NG
        NCH = CHS + CH0
        with nc.Block() as block:
            @block.sync
            def _(sp):
                def load(c, s):
                    sp.dma_start(RAW[s][:], w_chunks[bass.ds(c, 1)].rearrange("a p k n -> (a p) k n")).then_inc(w_loaded[s], 16)
                    sp.dma_start(SELF[s][:], sel_chunks[bass.ds(c, 1)].rearrange("a p n -> (a p) n")).then_inc(w_loaded[s], 16)
                load(0, 0)
                load(1, 1)
                with sp.Fori(1, NCH // 2) as k:
                    for s in range(2):
                        sp.wait_ge(down_done, (k * 2 + (s - 1)) * NG)
                        sp.nop(nofuse=True)
                        load(k * 2 + s, s)

            @block.gpsimd
            def _(pool):
                with pool.Fori(0, NCH // 2) as k:
                    for s in range(2):
                        pool.wait_ge(w_loaded[s], k * 32 + 32)
                        pool.nop(nofuse=True)
                        nc.gpsimd.tensor_copy(WH[s][:], RAW[s][:, 0:2, :]).then_inc(w_split[s], 1)
                        nc.gpsimd.tensor_copy(SEL[s][:], SELF[s][:]).then_inc(w_split[s], 1)
                        pool.wait_ge(w_split[s], k * 3 + 2)
                        nc.gpsimd.tensor_tensor(WL[s][:], RAW[s][:, 0:2, :], WH[s][:].bitcast(F32),
                                                ALU.subtract).then_inc(w_split[s], 1)

            @block.tensor
            def _(pe):
                def product(ps, s, i, cols):
                    nc.tensor.matmul(ps[:], WH[s][:, i, :], XH[:, cols], start=True, stop=False)
                    nc.tensor.matmul(ps[:], WH[s][:, i, :], XL[:, cols], start=False, stop=False)
                    return nc.tensor.matmul(ps[:], WL[s][:, i, :], XH[:, cols], start=False, stop=True)

                def down(n, s, g, start=False):
                    pe.wait_ge(h_ready, n + 1)
                    nc.tensor.matmul(acc[g][:], RAW[s][:, 2, :], HT[g % 2][:], start=start, stop=True,
                                     skip_group_check=True).then_inc(down_done, 1)

                def chunk(k, s, shared):
                    pe.wait_ge(w_split[s], k * 3 + 3)
                    for g in range(NG):
                        n = (k * 2 + s) * NG + g
                        peeled = isinstance(k, int)
                        cols = slice(g * GW, (g + 1) * GW)
                        if not (peeled and n < 2):
                            pe.wait_ge(silu_done, n - 1)
                        product(psG[g % 2], s, 0, cols).then_inc(gate_ready, 1)
                        if not (peeled and n < 1):
                            pe.wait_ge(mul_done, n)
                        product(psU, s, 1, cols).then_inc(up_ready, 1)
                        if not shared:
                            pe.wait_ge(h_ready, n)
                            nc.tensor.matmul(psR[:], SEL[s][:], GT[:, cols], start=True, stop=True).then_inc(weight_ready, 1)
                        if not (peeled and n < 1):
                            if g:
                                down(n - 1, s, g - 1, start=(shared and s == 0))
                            else:
                                down(n - 1, 1 - s, NG - 1, start=(shared and s == 1))

                pe.wait_ge(x_split, 2)
                chunk(0, 0, True)
                chunk(0, 1, True)
                with pe.Fori(1, NCH // 2) as k:
                    chunk(k, 0, False)
                    chunk(k, 1, False)
                down(NCH * NG - 1, 1, NG - 1)

            @block.scalar
            def _(act):
                def silu(n, g, free):
                    act.wait_ge(gate_ready, n + 1)
                    if free:
                        act.wait_ge(mul_done, n - 1)
                    nc.scalar.activation(SG[g % 2][:], psG[g % 2][:], ACT.Silu).then_inc(silu_done, 1)

                for n in range(NSH):
                    silu(n, n % NG, n >= 2)
                with act.Fori(1, NCH // 2) as k:
                    for i in range(2 * NG):
                        silu(k * (2 * NG) + i, i % NG, True)

            @block.vector
            def _(dve):
                nc.vector.tensor_copy(XH[:], X[:]).then_inc(x_split, 1)
                dve.wait_ge(x_split, 1)
                nc.vector.tensor_tensor(XL[:], X[:], XH[:].bitcast(F32), ALU.subtract).then_inc(x_split, 1)

                def hidden(n, g, shared, free):
                    dve.wait_ge(up_ready, n + 1)
                    dve.wait_ge(silu_done, n + 1)
                    nc.vector.tensor_tensor(T[g % 2][:], SG[g % 2][:], psU[:], ALU.mult).then_inc(mul_done, 1)
                    dve.wait_ge(mul_done, n + 1)
                    if free:
                        dve.wait_ge(down_done, n - 1)
                    if shared:
                        nc.vector.tensor_copy(HT[g % 2][:], T[g % 2][:]).then_inc(h_ready, 1)
                    else:
                        dve.wait_ge(weight_ready, n - (NSH - 1))
                        nc.vector.tensor_tensor(HT[g % 2][:], T[g % 2][:], psR[:], ALU.mult).then_inc(h_ready, 1)

                for n in range(NSH):
                    hidden(n, n % NG, True, n >= 2)
                with dve.Fori(1, NCH // 2) as k:
                    for i in range(2 * NG):
                        hidden(k * (2 * NG) + i, i % NG, False, True)
                dve.wait_ge(down_done, NCH * NG)
                for g in range(NG):
                    cols = slice(g * GW, (g + 1) * GW)
                    nc.vector.tensor_tensor(Y[:, cols], X[:, cols], acc[g][:], ALU.add).then_inc(y_done, 1)
                dve.wait_ge(y_done, NG)


def project_l1(nc, X, weights, decays, QS, KS, LATD):
    with ExitStack() as ctx:
        sb, pb, sem = sbuf(nc, ctx), psum(nc, ctx), Sems(nc, ctx)
        W = {n: sb(f"p1_{n}", list(w.shape), F32) for n, w in weights.items()}
        DEC = sb("p1_DEC", [P, 4, S], F32)
        kv, lat = sb("p1_kv", [P, GW], F32), sb("p1_lat", [DL, GW], F32)
        val = [sb(f"p1_val{m}", [P, GW], F32) for m in range(2)]
        rest = [sb(f"p1_rest{m}", [P, GW], F32) for m in range(2)]
        part = [[sb(f"p1_part{m}{i}", [P, GW], BF16) for i in range(NPART)] for m in range(2)]
        psQ, psKV, psL, psK = pb("p1_psQ"), pb("p1_psKV"), pb("p1_psL"), pb("p1_psK")
        loaded, q_ready, kv_ready, kv_read, lat_ready, lat_read, k_ready, val_done, rest_done, act_part, last_part, stored, lat_stored = (
            sem(f"p1_{n}") for n in ("loaded", "q_ready", "kv_ready", "kv_read", "lat_ready", "lat_read", "k_ready",
                                     "val_done", "rest_done", "act_part", "last_part", "stored", "lat_stored"))
        NV = 4
        STORES = (3, 3, 5, 5)
        BEFORE = (0, 3, 6, 11, 16)
        with nc.Block() as block:
            @block.sync
            def _(sp):
                for n, w in weights.items():
                    sp.dma_start(W[n][:], w).then_inc(loaded, 16)
                sp.dma_start(DEC[:], decays.partition_broadcast(P)).then_inc(loaded, 16)
                def group(g):
                    tok = bass.ds(g * GW, GW)
                    wait(sp, lat_read, g + 1)
                    sp.dma_start(LATD[:, tok], lat[:]).then_inc(lat_stored, 16)
                    for w in range(NV):
                        m = w % 2
                        wait(sp, last_part, g * NV + w + 1)
                        sp.nop(nofuse=True)
                        dst = (QS if w < 2 else KS)[w % 2]
                        for i in range(STORES[w]):
                            sp.dma_start(dst[:, i, :, tok], part[m][i % NPART][:]).then_inc(stored, 16)
                group(0)
                with sp.Fori(1, NG) as g:
                    group(g)
                sp.wait_ge(stored, NG * 16 * 16)
                sp.wait_ge(lat_stored, NG * 16)

            @block.tensor
            def _(pe):
                pe.wait_ge(loaded, 16 * (len(weights) + 1))
                def group(g):
                    xg = X[:, bass.ds(g * GW, GW)]
                    wait(pe, val_done, g * NV)
                    nc.tensor.matmul(psKV[:], W["wk"][:], xg, start=True, stop=False)
                    nc.tensor.matmul(psKV[:], W["wv"][:], xg, start=False, stop=True).then_inc(kv_ready, 1)
                    nc.tensor.matmul(psQ[:], W["wq"][:], xg, start=True, stop=True).then_inc(q_ready, 1)
                    wait(pe, kv_read, g + 1)
                    nc.tensor.matmul(psL[0:DL, :], W["down"][:], kv[:], start=True, stop=True).then_inc(lat_ready, 1)
                    wait(pe, lat_read, g + 1)
                    nc.tensor.matmul(psK[:], W["upk"][:], lat[:], start=True, stop=True).then_inc(k_ready, 1)
                group(0)
                with pe.Fori(1, NG) as g:
                    group(g)

            @block.scalar
            def _(act):
                def group(g):
                    wait(act, kv_ready, g + 1)
                    wait(act, lat_ready, g)
                    nc.scalar.activation(kv[:], psKV[:], ACT.Copy).then_inc(kv_read, 1)
                    wait(act, lat_ready, g + 1)
                    wait(act, k_ready, g)
                    wait(act, lat_stored, g * 16)
                    nc.scalar.activation(lat[:], psL[0:DL, :], ACT.Copy).then_inc(lat_read, 1)
                    for w in range(NV + 1):
                        if w < NV:
                            if w < 2:
                                wait(act, stored, g * 256)
                            else:
                                wait(act, stored, g * 256 + 16 * BEFORE[w - 1])
                            wait(act, val_done, g * NV + w + 1)
                            nc.scalar.activation(part[w % 2][0][:], val[w % 2][:], ACT.Copy).then_inc(act_part, 1)
                        if w:
                            wait(act, rest_done, g * NV + w)
                            nc.scalar.activation(part[(w - 1) % 2][1][:], rest[(w - 1) % 2][:], ACT.Copy).then_inc(act_part, 1)
                group(0)
                with act.Fori(1, NG) as g:
                    group(g)

            P1 = (1, 2, 4, 6)
            P2 = (3, 5, 7, 8)

            @block.vector
            def _(dve):
                dve.wait_ge(loaded, 16 * (len(weights) + 1))
                def group(g):
                    pos = bass.ds((g % 2) * GW, GW)
                    for w in range(NV + 1):
                        if w < NV:
                            if w == 0:
                                wait(dve, q_ready, g + 1)
                            if w == 2:
                                wait(dve, k_ready, g + 1)
                            if w < 2:
                                wait(dve, act_part, g * 8)
                                wait(dve, rest_done, g * NV)
                            else:
                                wait(dve, rest_done, g * NV + w - 1)
                            nc.vector.tensor_tensor(val[w % 2][:], (psQ if w < 2 else psK)[:], DEC[:, w, pos], ALU.mult).then_inc(val_done, 1)
                        if w:
                            v = w - 1
                            wait(dve, act_part, g * 8 + P1[v])
                            wait(dve, val_done, g * NV + v + 1)
                            if v < 2:
                                wait(dve, last_part, g * NV)
                            else:
                                wait(dve, last_part, g * NV + v - 1)
                            nc.vector.tensor_tensor(rest[v % 2][:], val[v % 2][:], part[v % 2][0][:], ALU.subtract).then_inc(rest_done, 1)
                group(0)
                with dve.Fori(1, NG) as g:
                    group(g)

            @block.gpsimd
            def _(pool):
                def group(g):
                    for w in range(NV):
                        wait(pool, act_part, g * 8 + P2[w])
                        nc.gpsimd.tensor_tensor(part[w % 2][2][:], rest[w % 2][:], part[w % 2][1][:], ALU.subtract).then_inc(last_part, 1)
                group(0)
                with pool.Fori(1, NG) as g:
                    group(g)


SLOTS1 = 3


def attention_l1(nc, upv, correct, ident16, QS, KS, LATD, OD):
    NT = KB + 1
    LAG = 2
    NS = NT * HQ * 2
    NM = KB * HQ * 2
    MS = NM + 4
    LOADS = (6 + 6 + 2) * 16
    assert NS % 3 == 0 and SLOTS1 * MS % 3 == 0
    with ExitStack() as ctx:
        sb, pb, sem = sbuf(nc, ctx), psum(nc, ctx), Sems(nc, ctx)
        QP = [sb(f"a1_QP{s}", [P, 2, HQ, S], BF16) for s in range(SLOTS1)]
        KP = [sb(f"a1_KP{s}", [P, 2, HQ, S], BF16) for s in range(SLOTS1)]
        LAT = [sb(f"a1_LAT{s}", [DL, S], F32) for s in range(SLOTS1)]
        WV = [sb(f"a1_WV{s}", [DL, P], F32) for s in range(SLOTS1)]
        V = [sb(f"a1_V{s}", [P, S], F32) for s in range(SLOTS1)]
        PR = [sb(f"a1_PR{r}", [P, HQ, S], F32) for r in range(3)]
        COR = sb("a1_COR", [P, 896], F32)
        junk = sb("a1_junk", [P, 2, GW], BF16)
        OST = sb("a1_OST", [P, S], F32)
        half_max = sb("a1_half_max", [P, HQ, KB, 2], F32)
        neg = sb("a1_neg", [P, HQ * KB], F32)
        neg_part = sb("a1_neg_part", [P, 2, HQ * KB], BF16)
        ID = sb("a1_ID", [P, P], BF16)
        MT = sb("a1_MT", [HQ * KB, 2, P], BF16)
        ring = [pb(f"a1_ring{r}") for r in range(3)]
        mring = [pb(f"a1_mring{r}") for r in range(3)]
        OUT = pb("a1_OUT", S)
        slot_set = [sem(f"slot_set{s}") for s in range(SLOTS1)]
        pack_loaded = [sem(f"pack_loaded{s}") for s in range(SLOTS1)]
        (cor_loaded, s_filled, s_read, m_filled, m_read, masked, pv_done, out_read, out_stored, neg_done, m_rows,
         v_set) = (sem(n) for n in ("cor_loaded", "s_filled", "s_read", "m_filled", "m_read", "masked", "pv_done",
                                    "out_read", "out_stored", "neg_done", "m_rows", "v_set"))

        def known(it):
            return isinstance(it, int)

        def score_cols(T):
            for a, b in pieces(0, T * P):
                yield a, b, T - 1, 0
            for a, b in pieces(T * P, S):
                yield a, b, T, 1

        def set_slot(eng, nc_eng, s):
            for n, (rows, value) in enumerate(((QP[s][64:96], 0.0), (QP[s][96:P], 0.0), (KP[s][64:96], BF16_ONES),
                                               (KP[s][96:P], 0.0))):
                if n:
                    eng.wait_ge(slot_set[s], n)
                nc_eng.memset(rows.bitcast(F32), value).then_inc(slot_set[s], 1)
            eng.wait_ge(slot_set[s], 4)

        with nc.Block() as block:
            @block.sync
            def _(sp):
                def load(b, q, s):
                    tok, heads = bass.ds(b * S, S), bass.ds(q * HQ, HQ)
                    got = pack_loaded[s]
                    for a in range(2):
                        for r in range(NPART):
                            rows = slice(r * 24, r * 24 + 24)
                            sp.dma_start(QP[s][rows, a], QS[a, heads, :, :, tok].rearrange("h i d t -> (i d) h t")).then_inc(got, 16)
                            sp.dma_start(KP[s][rows, a], KS[a, heads, r:r + 3, :, tok].rearrange("h i d t -> (i d) h t")).then_inc(got, 16)
                    sp.dma_start(LAT[s][:], LATD[:, tok]).then_inc(got, 16)
                    sp.dma_start(WV[s][:], upv[bass.ds(q, 1)].rearrange("a e n -> (a e) n")).then_inc(got, 16)

                def max_rows(it, s):
                    sp.wait_ge(m_read, it * MS + NM + 2)
                    for i in range(2):
                        for a in range(2):
                            sp.dma_start(QP[s][PAIRS + i:PAIRS + i + 1, a], MT[:, i, :]).then_inc(m_rows, 16)

                def store(it):
                    sp.wait_ge(out_read, it + 1)
                    sp.dma_start(OD[bass.ds(it, 1)].rearrange("a p t -> (a p) t"), OST[:]).then_inc(out_stored, 16)

                sp.dma_start(COR[:], correct).then_inc(cor_loaded, 16)
                sp.dma_start(ID[:], ident16).then_inc(cor_loaded, 16)
                for s in range(SLOTS1):
                    sp.wait_ge(slot_set[s], 4)
                    load(0, s, s)
                max_rows(0, 0)
                max_rows(1, 1)

                def refill(it, b, q, s):
                    sp.wait_ge(s_read, it * NS + NS)
                    load(b, q, s)

                refill(0, 0, 3, 0)
                for it in range(1, NIT):
                    store(it - 1)
                    if it + 1 < NIT:
                        max_rows(it + 1, (it + 1) % SLOTS1)
                    if it + 3 < NIT:
                        refill(it, (it + 3) // NQUAD, (it + 3) % NQUAD, it % SLOTS1)
                store(NIT - 1)
                sp.wait_ge(out_stored, NIT * 16)

            @block.gpsimd
            def _(pool):
                set_slot(pool, nc.gpsimd, 1)

                with pool.Fori(0, NIT) as it:
                    for T in range(NT):
                        for j in range(HQ):
                            pool.wait_ge(s_read, it * NS + (T * HQ + j + 1) * 2)
                            pool.nop(nofuse=True)
                            if T:
                                d = PR[T % 3][:, j, (T - 1) * P:T * P]
                                last = nc.gpsimd.affine_select(out=d, in_=d, compare_op=ALU.is_ge, fill=0.0, base=0,
                                                               pattern=[[-1, P]], channel_multiplier=1)
                            if T < KB:
                                d = PR[T % 3][:, j, T * P:(T + 1) * P]
                                last = nc.gpsimd.affine_select(out=d, in_=d, compare_op=ALU.is_gt, fill=0.0, base=0,
                                                               pattern=[[1, P]], channel_multiplier=-1)
                            last.then_inc(masked, 1)

            @block.tensor
            def _(pe):
                def ring_free(it, i):
                    if not known(it) or it * MS + i >= 3:
                        pe.wait_ge(m_read, it * MS + (i - 2))

                def max_scores(it, i, s):
                    sb_, j, half = i // (2 * HQ), (i // 2) % HQ, i % 2
                    ring_free(it, i)
                    t0 = half * GW
                    split = min(max((sb_ + 1) * P, t0), t0 + GW)
                    for a, b, var in ((t0, split, 1), (split, t0 + GW, 0)):
                        if a < b:
                            last = nc.tensor.matmul(mring[(s * MS + i) % 3][:, a - t0:b - t0],
                                                    QP[s][0:PAIRS, var, j, sb_ * P:(sb_ + 1) * P],
                                                    KP[s][0:PAIRS, var, j, a:b], start=True, stop=True)
                    last.then_inc(m_filled, 1)

                def turn_max(it, i, s):
                    part = i - NM
                    if part == 0:
                        pe.wait_ge(neg_done, it * 4 + 4)
                    ring_free(it, i)
                    nc.tensor.transpose(mring[(s * MS + i) % 3][0:HQ * KB, 0:P // 2].bitcast(BF16), neg_part[:, part, :], ID[:]).then_inc(m_filled, 1)

                def values(it, i, s):
                    ring_free(it, i)
                    half = i - NM - 2
                    for n in range(4):
                        kb = half * 4 + n
                        last = nc.tensor.matmul(mring[(s * MS + i) % 3][:, n * P:(n + 1) * P], LAT[s][:, kb * P:(kb + 1) * P], WV[s][:],
                                                start=True, stop=True)
                    last.then_inc(m_filled, 1)

                def scores(it, T, j, half, s):
                    n = (T * HQ + j) * 2 + half
                    if n == 0:
                        pe.wait_ge(m_rows, it * 64 + 64)
                    if not known(it) or it * NS + n >= 3:
                        pe.wait_ge(s_read, it * NS + (n - 2))
                    for a, b, kb, var in score_cols(T):
                        if a // GW == half:
                            last = nc.tensor.matmul(ring[n % 3][:, a - half * GW:b - half * GW],
                                                    KP[s][:, var, j, kb * P:(kb + 1) * P], QP[s][:, var, j, a:b],
                                                    start=True, stop=True)
                    last.then_inc(s_filled, 1)

                def weigh(it, T, s, quarter):
                    if quarter == 0:
                        pe.wait_ge(masked, it * (NT * HQ) + (T + 1) * HQ)
                        if T == 0:
                            pe.wait_ge(m_read, it * MS + MS)
                            if not known(it) or it > 0:
                                pe.wait_ge(out_read, it)
                    q0, q1 = quarter * (GW // 2), (quarter + 1) * (GW // 2)
                    for a, b, kb, var in score_cols(T):
                        a, b = max(a, q0), min(b, q1)
                        if a < b:
                            for j in range(HQ):
                                last = nc.tensor.matmul(OUT[j * HP:(j + 1) * HP, a:b],
                                                        V[s][:, kb * P + j * HP:kb * P + (j + 1) * HP],
                                                        PR[T % 3][:, j, a:b], start=(T == 0 and a % GW == 0),
                                                        stop=(T == NT - 1), skip_group_check=True)
                    if quarter == 3:
                        last.then_inc(pv_done, 1)

                def pair(it, s, last_pair):
                    s1 = (s + 1) % SLOTS1
                    issued = 0
                    maxima = (NT - LAG - 1) * HQ * 2
                    for T in range(NT):
                        for j in range(HQ):
                            for half in range(2):
                                if T + LAG < NT:
                                    scores(it, T + LAG, j, half, s)
                                elif not last_pair:
                                    scores(it + 1, T + LAG - NT, j, half, s1)
                                if last_pair:
                                    continue
                                want = min(NM, -(-NM * ((T * HQ + j) * 2 + half + 1) // maxima))
                                while issued < want:
                                    max_scores(it + 1, issued, s1)
                                    issued += 1
                            if T == NT - LAG - 1 and not last_pair:
                                if j < 2:
                                    turn_max(it + 1, NM + j, s1)
                                else:
                                    values(it + 1, NM + j, s1)
                            for quarter in {0: (), 1: (), 2: (0, 1), 3: (2, 3)}[j] if T == 0 else (j,):
                                weigh(it, T, s, quarter)

                def packs(it_count, s):
                    pe.wait_ge(pack_loaded[s], it_count)

                pe.wait_ge(cor_loaded, 32)
                packs(LOADS, 0)
                for i in range(NM):
                    max_scores(0, i, 0)
                turn_max(0, NM, 0)
                turn_max(0, NM + 1, 0)
                values(0, NM + 2, 0)
                values(0, NM + 3, 0)
                for T in range(LAG):
                    for j in range(HQ):
                        for half in range(2):
                            scores(0, T, j, half, 0)
                packs(LOADS, 1)
                pair(0, 0, False)
                with pe.Fori(0, 2) as k:
                    for r in range(SLOTS1):
                        nxt = (r + 2) % SLOTS1
                        pe.wait_ge(pack_loaded[nxt], k * LOADS + LOADS * (1 + (r + 2) // SLOTS1))
                        pair(k * 3 + (r + 1), (r + 1) % SLOTS1, False)
                pair(NIT - 1, (NIT - 1) % SLOTS1, True)

            @block.scalar
            def _(act):
                def pair(it):
                    for T in range(NT):
                        for i in range(2 * HQ):
                            n, half = T * HQ * 2 + i, i % 2
                            act.wait_ge(s_filled, it * NS + (n + 1))
                            if i == 0 and not (known(it) and T < 3):
                                act.wait_ge(pv_done, it * NT + (T - 2))
                            nc.scalar.activation(PR[T % 3][:, i // 2, half * GW:(half + 1) * GW], ring[n % 3][:],
                                                 ACT.Exp).then_inc(s_read, 1)
                pair(0)
                with act.Fori(1, NIT) as it:
                    pair(it)

            @block.vector
            def _(dve):
                def take_max(it, i, s):
                    sb_, j, half = i // (2 * HQ), (i // 2) % HQ, i % 2
                    dve.wait_ge(m_filled, it * MS + (i + 1))
                    out = half_max[:, j, sb_, half:half + 1]
                    if sb_ // 4 == half:
                        c = 384 - (sb_ % 4) * P
                        dve.nop(nofuse=True)
                        nc.vector.tensor_tensor_reduce(out=junk[:, j % 2, :], in0=mring[(s * MS + i) % 3][:], in1=COR[:, c:c + GW], scale=1.0,
                                                       scalar=-3.0e38, op0=ALU.mult, op1=ALU.max, accum_out=out).then_inc(m_read, 1)
                    else:
                        nc.vector.tensor_reduce(out, mring[(s * MS + i) % 3][:], AX.X, ALU.max).then_inc(m_read, 1)

                def finish_max(it, s):
                    dve.wait_ge(m_read, it * MS + NM)
                    hm = half_max[:].rearrange("p j b a -> p (j b) a")
                    nc.vector.tensor_reduce(neg[:], hm, AX.X, ALU.max).then_inc(neg_done, 1)
                    dve.wait_ge(neg_done, it * 4 + 1)
                    nc.vector.tensor_scalar(neg[:], neg[:], -1.0, None, ALU.mult).then_inc(neg_done, 1)
                    dve.wait_ge(neg_done, it * 4 + 2)
                    nc.vector.tensor_copy(neg_part[:, 0, :], neg[:]).then_inc(neg_done, 1)
                    dve.wait_ge(neg_done, it * 4 + 3)
                    nc.vector.tensor_tensor(neg_part[:, 1, :], neg[:], neg_part[:, 0, :], ALU.subtract).then_inc(neg_done, 1)
                    if not known(it) or it > 0:
                        dve.wait_ge(m_rows, it * 64)
                    for part in range(2):
                        i = NM + part
                        dve.wait_ge(m_filled, it * MS + (i + 1))
                        nc.vector.tensor_copy(MT[:, part, :], mring[(s * MS + i) % 3][0:HQ * KB, 0:P // 2].bitcast(BF16)).then_inc(m_read, 1)
                    if not known(it) or it > 2:
                        dve.wait_ge(pv_done, (it - 2) * NT)
                    for half in range(2):
                        i = NM + 2 + half
                        dve.wait_ge(m_filled, it * MS + (i + 1))
                        heads = V[s][:].rearrange("p (n c) -> p n c", c=HP)[:, half * 16:half * 16 + 16, 0:HD]
                        src = mring[(s * MS + i) % 3][:].rearrange("p (n c) -> p n c", c=HP)[:, :, 0:HD]
                        nc.vector.tensor_copy(heads, src).then_inc(m_read, 1)

                def copy_out(it):
                    dve.wait_ge(pv_done, it * NT + NT)
                    if not known(it) or it > 0:
                        dve.wait_ge(out_stored, it * 16)
                    nc.vector.tensor_copy(OST[:], OUT[:]).then_inc(out_read, 1)

                def pair(it, s, first, last_pair):
                    for i in range(NM):
                        if i == 2 and not first:
                            copy_out(it - 1)
                        if not last_pair:
                            take_max(it + 1, i, (s + 1) % SLOTS1)
                    if not last_pair:
                        finish_max(it + 1, (s + 1) % SLOTS1)

                set_slot(dve, nc.vector, 0)
                for s in range(SLOTS1):
                    nc.vector.memset(V[s][:], 0.0).then_inc(v_set, 1)
                dve.wait_ge(v_set, SLOTS1)
                for s in range(SLOTS1):
                    ones = V[s][:].rearrange("p (n c) -> p n c", c=HP)[:, :, HD:HD + 1]
                    nc.vector.memset(ones, 1.0).then_inc(v_set, 1)
                dve.wait_ge(v_set, 2 * SLOTS1)
                set_slot(dve, nc.vector, 2)
                dve.wait_ge(cor_loaded, 32)
                for i in range(NM):
                    take_max(0, i, 0)
                finish_max(0, 0)
                pair(0, 0, True, False)
                with dve.Fori(0, 2) as k:
                    for r in range(SLOTS1):
                        pair(k * 3 + (r + 1), (r + 1) % SLOTS1, False, False)
                pair(NIT - 1, (NIT - 1) % SLOTS1, False, True)
                copy_out(NIT - 1)


def normalise(nc, OD, OALL, den_pick, consts):
    with ExitStack() as ctx:
        sb, pb, sem = sbuf(nc, ctx), psum(nc, ctx), Sems(nc, ctx)
        pick = sb("n_pick", [P, HQ], F32)
        rec = sb("n_rec", [P, NIT * KB, HQ], F32)
        psD = pb("n_psD")
        psB = [pb(f"n_psB{r}") for r in range(4)]
        loaded, pick_loaded, dens, inverse, spread, scaled = (
            sem(f"n_{n}") for n in ("loaded", "pick_loaded", "dens", "inverse", "spread", "scaled"))
        with nc.Block() as block:
            @block.sync
            def _(sp):
                sp.dma_start(pick[:], den_pick).then_inc(pick_loaded, 16)
                for it in range(NIT):
                    sp.dma_start(OALL[:, it, :], OD[it]).then_inc(loaded, 16)

            @block.tensor
            def _(pe):
                pe.wait_ge(pick_loaded, 16)
                pe.wait_ge(loaded, 16 * NIT)
                for it in range(NIT):
                    for kb in range(KB):
                        n = it * KB + kb
                        last = nc.tensor.matmul(psD[:, n * HQ:(n + 1) * HQ], OALL[:, it, kb * P:(kb + 1) * P], pick[:],
                                                start=True, stop=True)
                last.then_inc(dens, 1)
                pe.wait_ge(inverse, 1)
                for u in range(2 * NIT):
                    if u >= 4:
                        pe.wait_ge(scaled, u - 3)
                    for n in range(4):
                        for j in range(HQ):
                            col = rec[:, u * 4 + n, j:j + 1].to_broadcast([P, HP])
                            last = nc.tensor.matmul(psB[u % 4][j * HP:(j + 1) * HP, n * P:(n + 1) * P], col,
                                                    consts["ident"][:], start=True, stop=True)
                    last.then_inc(spread, 1)

            @block.vector
            def _(dve):
                dve.wait_ge(dens, 1)
                nc.vector.reciprocal(rec[:].rearrange("p n j -> p (n j)"), psD[:, 0:NIT * KB * HQ]).then_inc(inverse, 1)
                for u in range(2 * NIT):
                    dve.wait_ge(spread, u + 1)
                    o = OALL[:, u // 2, (u % 2) * GW:(u % 2 + 1) * GW]
                    nc.vector.tensor_tensor(o, o, psB[u % 4][:], ALU.mult).then_inc(scaled, 1)
                dve.wait_ge(scaled, 2 * NIT)


G1 = 32


def route_l1(nc, X, wr, earlier, consts, GT):
    with ExitStack() as ctx:
        sb, pb, sem = sbuf(nc, ctx), psum(nc, ctx), Sems(nc, ctx)
        W = sb("r1_W", [P, NE1], F32)
        tri = sb("r1_tri", [P, NE1, NE1], F32)
        lg, pr = sb("r1_lg", [P, NT_TOK, NE1], F32), sb("r1_pr", [P, NT_TOK, NE1], F32)
        sm = sb("r1_sm", [P, NT_TOK], F32)
        t1, t2 = (sb(f"r1_{n}", [P, NT_TOK, NE1, NE1], F32) for n in ("t1", "t2"))
        gates = sb("r1_gates", [P, NT_TOK, 2, G1], F32)
        psL = pb("r1_psL")
        psT = [pb(f"r1_psT{g}") for g in range(NG)]
        loaded, logits, shifted, exped, step, copied, turned = (
            sem(f"r1_{n}") for n in ("loaded", "logits", "shifted", "exped", "step", "copied", "turned"))
        with nc.Block() as block:
            @block.sync
            def _(sp):
                sp.dma_start(W[:], wr).then_inc(loaded, 16)
                sp.dma_start(tri[:], earlier.partition_broadcast(P)).then_inc(loaded, 16)

            @block.tensor
            def _(pe):
                pe.wait_ge(loaded, 32)
                for t in range(NT_TOK):
                    last = nc.tensor.matmul(psL[:, t * NE1:(t + 1) * NE1], X[:, t * P:(t + 1) * P], W[:], start=True, stop=True)
                last.then_inc(logits, 1)
                pe.wait_ge(copied, 2)
                for t in range(NT_TOK):
                    last = nc.tensor.transpose(psT[t // 4][0:2 * G1, (t % 4) * P:(t % 4 + 1) * P],
                                               gates[:, t].rearrange("p a e -> p (a e)"), consts["ident"][:])
                    if t % 4 == 3:
                        last.then_inc(turned, 1)

            @block.scalar
            def _(act):
                act.wait_ge(shifted, 1)
                nc.scalar.activation(pr[:], lg[:], ACT.Exp).then_inc(exped, 1)

            @block.vector
            def _(dve):
                n = [0]

                def link(ins):
                    n[0] += 1
                    ins.then_inc(step, 1)
                    dve.wait_ge(step, n[0])

                v = nc.vector
                wide = lambda t: t.unsqueeze(2).to_broadcast([P, NT_TOK, NE1])
                link(v.memset(gates[:], 0.0))
                for a in range(2):
                    link(v.memset(gates[:, :, a, NE1:NE1 + 1], 1.0))
                dve.wait_ge(loaded, 32)
                dve.wait_ge(logits, 1)
                psl = psL[:, 0:NT_TOK * NE1].rearrange("p (t e) -> p t e", e=NE1)
                link(v.tensor_reduce(sm[:], psl, AX.X, ALU.max))
                v.tensor_tensor(lg[:], psl, wide(sm[:]), ALU.subtract).then_inc(shifted, 1)
                dve.wait_ge(exped, 1)
                link(v.tensor_reduce(sm[:], pr[:], AX.X, ALU.add))
                link(v.reciprocal(sm[:], sm[:]))
                link(v.tensor_tensor(pr[:], pr[:], wide(sm[:]), ALU.mult))
                other = pr[:].unsqueeze(2).to_broadcast([P, NT_TOK, NE1, NE1])
                own = pr[:].unsqueeze(3).to_broadcast([P, NT_TOK, NE1, NE1])
                link(v.tensor_tensor(t1[:], other, own, ALU.is_gt))
                link(v.tensor_tensor(t2[:], other, own, ALU.is_equal))
                link(v.tensor_tensor(t2[:], t2[:], tri[:].unsqueeze(1).to_broadcast([P, NT_TOK, NE1, NE1]), ALU.mult))
                link(v.tensor_tensor(t1[:], t1[:], t2[:], ALU.add))
                link(v.tensor_reduce(lg[:], t1[:], AX.X, ALU.add))
                link(v.tensor_scalar(lg[:], lg[:], 2.0, None, ALU.is_lt))
                link(v.tensor_tensor(pr[:], pr[:], lg[:], ALU.mult))
                link(v.tensor_reduce(sm[:], pr[:], AX.X, ALU.add))
                link(v.reciprocal(sm[:], sm[:]))
                for a in range(2):
                    v.tensor_tensor(gates[:, :, a, 0:NE1], pr[:], wide(sm[:]), ALU.mult).then_inc(copied, 1)
                for g in range(NG):
                    dve.wait_ge(turned, g + 1)
                    cols = slice(g * GW, (g + 1) * GW)
                    link(v.tensor_copy(GT[:, cols], psT[g][0:2 * G1, :]))
                    link(v.tensor_tensor(GT[G1:2 * G1, cols], psT[g][G1:2 * G1, :], GT[G1:2 * G1, cols].bitcast(F32), ALU.subtract))


def experts_l1(nc, X, Y, GT, w_experts, sel_experts, bias_fc, bias_proj):
    NX = NE1 + 1
    SE = NG * CH1
    with ExitStack() as ctx:
        sb, pb, sem = sbuf(nc, ctx), psum(nc, ctx), Sems(nc, ctx)
        XH, XL = sb("e1_XH", [P, TOK], F32R), sb("e1_XL", [P, TOK], F32R)
        RAW = [sb(f"e1_RAW{s}", [P, 2, HID], F32) for s in range(2)]
        WH = [sb(f"e1_WH{s}", [P, HID], F32R) for s in range(2)]
        WL = [sb(f"e1_WL{s}", [P, HID], F32R) for s in range(2)]
        SELF = [sb(f"e1_SELF{s}", [2 * G1, P], F32) for s in range(2)]
        SEL = [sb(f"e1_SEL{s}", [2 * G1, P], F32R) for s in range(2)]
        BF = sb("e1_BF", [P, NX * CH1], F32)
        BP = sb("e1_BP", [2 * G1, P], F32)
        GL = [sb(f"e1_GL{s}", [P, GW], F32) for s in range(2)]
        HT = [sb(f"e1_H{s}", [P, GW], F32) for s in range(2)]
        acc = [pb(f"e1_acc{g}") for g in range(NG)]
        psF = [pb(f"e1_psF{s}") for s in range(2)]
        psR = [pb(f"e1_psR{s}") for s in range(2)]
        x_split, bias_loaded = sem("x_split"), sem("bias_loaded")
        w_loaded = [sem(f"w_loaded{s}") for s in range(2)]
        w_split = [sem(f"w_split{s}") for s in range(2)]
        hid_ready, gate_ready, gelu_done, h_ready, down_done, y_done = (
            sem(n) for n in ("hid_ready", "gate_ready", "gelu_done", "h_ready", "down_done", "y_done"))
        with nc.Block() as block:
            @block.sync
            def _(sp):
                def load(e, s):
                    sp.dma_start(RAW[s][:], w_experts[bass.ds(e, 1)].rearrange("a p k n -> (a p) k n")).then_inc(w_loaded[s], 16)
                    sp.dma_start(SELF[s][:], sel_experts[bass.ds(e, 1)].rearrange("a p n -> (a p) n")).then_inc(w_loaded[s], 16)
                load(0, 0)
                sp.dma_start(BF[:], bias_fc).then_inc(bias_loaded, 16)
                sp.dma_start(BP[:], bias_proj).then_inc(bias_loaded, 16)
                load(1, 1)
                sp.wait_ge(down_done, SE)
                load(2, 0)
                with sp.Fori(1, NX // 2) as k:
                    for r in range(2):
                        sp.wait_ge(down_done, (k * 2 + r) * SE)
                        sp.nop(nofuse=True)
                        load(k * 2 + (r + 1), 1 - r)

            @block.gpsimd
            def _(pool):
                def split(count, s):
                    pool.wait_ge(w_loaded[s], count * 32 + 32)
                    pool.nop(nofuse=True)
                    nc.gpsimd.tensor_copy(WH[s][:], RAW[s][:, 0, :]).then_inc(w_split[s], 1)
                    nc.gpsimd.tensor_copy(SEL[s][:], SELF[s][:]).then_inc(w_split[s], 1)
                    pool.wait_ge(w_split[s], count * 3 + 2)
                    nc.gpsimd.tensor_tensor(WL[s][:], RAW[s][:, 0, :], WH[s][:].bitcast(F32), ALU.subtract).then_inc(w_split[s], 1)
                split(0, 0)
                with pool.Fori(0, NX // 2) as k:
                    split(k, 1)
                    split(k + 1, 0)

            @block.tensor
            def _(pe):
                def down(n, s, i):
                    g, c = i // CH1, i % CH1
                    pe.wait_ge(h_ready, n + 1)
                    nc.tensor.matmul(acc[g][:], RAW[s][:, 1, c * P:(c + 1) * P], HT[i % 2][:], start=False, stop=True,
                                     skip_group_check=True).then_inc(down_done, 1)

                def expert(e, count, s):
                    peeled = isinstance(e, int)
                    pe.wait_ge(w_split[s], count * 3 + 3)
                    for i in range(SE):
                        n = e * SE + i
                        g, c = i // CH1, i % CH1
                        cols = slice(g * GW, (g + 1) * GW)
                        if c == 0:
                            if not (peeled and i < 2 * CH1):
                                pe.wait_ge(h_ready, e * SE + (i - CH1))
                            nc.tensor.matmul(psR[g % 2][:], SEL[s][:], GT[:, cols], start=True, stop=True).then_inc(gate_ready, 1)
                        if not (peeled and i < 2):
                            pe.wait_ge(gelu_done, n - 1)
                        nc.tensor.matmul(psF[i % 2][:], WH[s][:, c * P:(c + 1) * P], XH[:, cols], start=True, stop=False)
                        nc.tensor.matmul(psF[i % 2][:], WH[s][:, c * P:(c + 1) * P], XL[:, cols], start=False, stop=False)
                        nc.tensor.matmul(psF[i % 2][:], WL[s][:, c * P:(c + 1) * P], XH[:, cols], start=False, stop=True)\
                            .then_inc(hid_ready, 1)
                        if not (peeled and i < 1):
                            down(n - 1, s if i else 1 - s, (i - 1) % SE)

                pe.wait_ge(bias_loaded, 32)
                for g in range(NG):
                    nc.tensor.matmul(acc[g][:], BP[:], GT[:, g * GW:(g + 1) * GW].bitcast(F32), start=True, stop=True)
                pe.wait_ge(x_split, 2)
                expert(0, 0, 0)
                with pe.Fori(0, NX // 2) as k:
                    expert(k * 2 + 1, k, 1)
                    expert(k * 2 + 2, k + 1, 0)
                down(NX * SE - 1, 0, SE - 1)

            @block.scalar
            def _(act):
                act.wait_ge(bias_loaded, 32)

                def gelu(e, i, free):
                    n = e * SE + i
                    act.wait_ge(hid_ready, n + 1)
                    if free:
                        act.wait_ge(h_ready, n - 1)
                    act.nop(nofuse=True)
                    nc.scalar.activation(GL[i % 2][:], psF[i % 2][:], ACT.Gelu_apprx_tanh,
                                         bias=BF[:, bass.ds(e * CH1 + i % CH1, 1)]).then_inc(gelu_done, 1)
                for i in range(SE):
                    gelu(0, i, i >= 2)
                with act.Fori(1, NX) as e:
                    for i in range(SE):
                        gelu(e, i, True)

            @block.vector
            def _(dve):
                nc.vector.tensor_copy(XH[:], X[:]).then_inc(x_split, 1)
                dve.wait_ge(x_split, 1)
                nc.vector.tensor_tensor(XL[:], X[:], XH[:].bitcast(F32), ALU.subtract).then_inc(x_split, 1)

                def hidden(e, i, free):
                    n = e * SE + i
                    if i % CH1 == 0:
                        dve.wait_ge(gate_ready, e * NG + (i // CH1 + 1))
                    dve.wait_ge(gelu_done, n + 1)
                    if free:
                        dve.wait_ge(down_done, n - 1)
                    nc.vector.tensor_tensor(HT[i % 2][:], GL[i % 2][:], psR[(i // CH1) % 2][:], ALU.mult).then_inc(h_ready, 1)
                for i in range(SE):
                    hidden(0, i, i >= 2)
                with dve.Fori(1, NX) as e:
                    for i in range(SE):
                        hidden(e, i, True)
                dve.wait_ge(down_done, NX * SE)
                for g in range(NG):
                    cols = slice(g * GW, (g + 1) * GW)
                    nc.vector.tensor_tensor(Y[:, cols], X[:, cols], acc[g][:], ALU.add).then_inc(y_done, 1)
                dve.wait_ge(y_done, NG)


def build(nc, a, out):
    q0 = nc.dram_tensor("q0_parts", (H, NPART, HD, TOK), BF16).ap()
    k0 = nc.dram_tensor("k0_parts", (H, NPART + 2, HD, TOK), BF16).ap()
    qn0 = nc.dram_tensor("q0_norm_parts", (H, NPART, TOK), BF16).ap()
    kn0 = nc.dram_tensor("k0_norm_parts", (H, NPART, TOK), BF16).ap()
    q1 = nc.dram_tensor("q1_parts", (2, H, NPART, HD, TOK), BF16).ap()
    k1 = nc.dram_tensor("k1_parts", (2, H, NPART + 2, HD, TOK), BF16).ap()
    lat = nc.dram_tensor("latent", (DL, TOK), F32).ap()
    o1 = nc.dram_tensor("o1_sums", (NIT, P, S), F32).ap()
    with ExitStack() as ctx:
        sb = sbuf(nc, ctx)
        X = sb("X", [P, TOK], F32)
        mean_of, ident = sb("mean_of", [P, P], F32), sb("ident", [P, P], F32)
        consts = dict(mean_of=mean_of, ident=ident)
        loaded, stored = Sems(nc, ctx)("x_loaded"), Sems(nc, ctx)("out_stored_all")
        with nc.Block() as block:
            @block.sync
            def _(sp):
                for tile, src in ((X, a["xT"]), (mean_of, a["mean_of"]), (ident, a["ident"])):
                    sp.dma_start(tile[:], src).then_inc(loaded, 16)
                sp.wait_ge(loaded, 48)

        def output_terms(quads, OALL):
            def terms(g):
                b, half = g // 2, g % 2
                return [(quads[:, q, :], OALL[:, b * NQUAD + q, half * GW:(half + 1) * GW]) for q in range(NQUAD)]
            return terms

        project_l0(nc, X, a["wq0"], a["wk0"], a["head_sum"], q0, k0, qn0, kn0)
        with ExitStack() as part:
            OALL = sbuf(nc, part)("OALL0", [P, NIT, S], F32)
            attention_l0(nc, a["xT"], a["wv0"], a["gamma"], q0, k0, qn0, kn0, OALL)
            Y, WO = sbuf(nc, part)("Y_a0", [P, TOK], F32), sbuf(nc, part)("WO0", [P, NQUAD, P], F32)
            add_and_norm(nc, "n0a", X, Y, consts, output_terms(WO, OALL), ((WO[:], a["wo0"].rearrange("q p n -> p q n")),))
        with ExitStack() as part:
            Y, GT = sbuf(nc, part)("Y_m0", [P, TOK], F32), sbuf(nc, part)("GT0", [P, TOK], F32R)
            route_l0(nc, X, a["gate_w"], a["gate_bias"], a["earlier"], consts, GT)
            experts_l0(nc, X, Y, GT, a["w_chunks"], a["sel_chunks"])
            add_and_norm(nc, "n0m", X, Y, consts)
        project_l1(nc, X, {n: a[n] for n in ("wq", "wk", "wv", "down", "upk")}, a["decays"], q1, k1, lat)
        attention_l1(nc, a["upv"], a["correct"], a["ident16"], q1, k1, lat, o1)
        with ExitStack() as part:
            OALL = sbuf(nc, part)("OALL1", [P, NIT, S], F32)
            normalise(nc, o1, OALL, a["den_pick"], consts)
            Y, WO = sbuf(nc, part)("Y_a1", [P, TOK], F32), sbuf(nc, part)("WO1", [P, NQUAD, P], F32)
            add_and_norm(nc, "n1a", X, Y, consts, output_terms(WO, OALL), ((WO[:], a["wo1"].rearrange("q p n -> p q n")),))
        with ExitStack() as part:
            Y, GT = sbuf(nc, part)("Y_m1", [P, TOK], F32), sbuf(nc, part)("GT1", [2 * G1, TOK], F32R)
            route_l1(nc, X, a["wr"], a["earlier"], consts, GT)
            experts_l1(nc, X, Y, GT, a["w_experts"], a["sel_experts"], a["bias_fc"], a["bias_proj"])
            add_and_norm(nc, "n1m", X, Y, consts)
        with nc.Block() as block:
            @block.sync
            def _(sp):
                sp.dma_start(out, X[:]).then_inc(stored, 16)
                sp.wait_ge(stored, 16)


def kernel(**inputs):
    import concourse.bacc as bacc
    import ml_dtypes
    from concourse.bass_utils import run_bass_kernel_spmd

    w = {n: np.asarray(v) for n, v in inputs.items()}

    def by_quad(m):
        o = np.zeros((NQUAD, m.shape[0], HQ, HP), m.dtype)
        o[..., :HD] = m.reshape(m.shape[0], NQUAD, HQ, HD).transpose(1, 0, 2, 3)
        return o.reshape(NQUAD, m.shape[0], P)

    def stacked(routed, shared):
        o = np.zeros((CHS + CH0, P, P), routed.dtype)
        o.reshape(-1, P)[:SHI] = shared
        o.reshape(-1, P)[CHS * P:] = routed.reshape(-1, P)
        return o

    gate = stacked(w["L0_ffn_Wg"], w["L0_ffn_Sg"]).transpose(0, 2, 1)
    up = stacked(w["L0_ffn_Wu"], w["L0_ffn_Su"]).transpose(0, 2, 1)
    down = stacked(w["L0_ffn_Wd"].transpose(0, 2, 1), w["L0_ffn_Sd"].T)
    sel0 = np.zeros((CHS + CH0, 2, NE0, P), np.float32)
    rows = np.arange(CH0 * P)
    sel0[CHS + rows // P, :, rows // I0, rows % P] = 1
    first = np.concatenate([w["L1_ffn_Wfc"], w["L1_ffn_Wfc_s"][None]])
    second = np.concatenate([w["L1_ffn_Wproj"], w["L1_ffn_Wproj_s"][None]])
    second = second.reshape(NE1 + 1, CH1, P, P).transpose(0, 2, 1, 3).reshape(NE1 + 1, P, HID)
    bias_fc = np.concatenate([w["L1_ffn_bfc"], w["L1_ffn_bfc_s"][None]]).reshape(-1, P).T
    bias_proj = np.zeros((2, G1, P), np.float32)
    bias_proj[:, :NE1 + 1] = np.concatenate([w["L1_ffn_bproj"], w["L1_ffn_bproj_s"][None]])
    sel1 = np.zeros((NE1 + 1, 2, G1, P), np.float32)
    for e in range(NE1 + 1):
        sel1[e, :, e] = 1
    pos = DECAY * (np.arange(S) - S // 2)
    scale = E ** -0.5
    decays = np.stack([scale * np.exp(pos), scale * np.exp(-pos), np.exp(-pos), np.exp(pos)])
    correct = np.ones((P, 896))
    row, col = np.arange(P)[:, None], np.arange(P)[None, :]
    correct[:, 384:512] = np.exp(-2 * DECAY * np.maximum(col - row, 0))
    den_pick = np.zeros((HQ, HP, HQ), np.float32)
    for j in range(HQ):
        den_pick[j, HD, j] = 1
    arrays = {
        "xT": w["L0_attn_q"].reshape(TOK, E).T,
        "wq0": w["L0_attn_Wq"], "wk0": w["L0_attn_Wk"], "wv0": by_quad(w["L0_attn_Wv"]),
        "wo0": by_quad(w["L0_attn_Wo"].T).transpose(0, 2, 1), "gamma": w["L0_attn_gamma"],
        "head_sum": np.repeat(np.eye(H), HD, 0).astype(np.float32),
        "gate_w": w["L0_ffn_gate_w"].T, "gate_bias": w["L0_ffn_gate_bias"],
        "earlier": np.tril(np.ones((NGRP, NGRP)), -1).astype(np.float32),
        "w_chunks": np.stack([gate, up, down], 2), "sel_chunks": sel0.reshape(-1, P, P),
        "wq": w["L1_attn_W_q"], "wk": w["L1_attn_W_k"], "wv": w["L1_attn_W_v"], "down": w["L1_attn_W_down_kv"],
        "upk": w["L1_attn_W_up_k"], "upv": by_quad(w["L1_attn_W_up_v"]),
        "wo1": by_quad(w["L1_attn_W_o"].T).transpose(0, 2, 1), "decays": decays.astype(np.float32),
        "correct": correct.astype(np.float32), "ident16": np.eye(P).astype(ml_dtypes.bfloat16),
        "ident": np.eye(P).astype(np.float32), "mean_of": np.full((P, P), 1 / E, np.float32),
        "den_pick": den_pick.reshape(P, HQ), "wr": w["L1_ffn_Wr"],
        "w_experts": np.stack([first, second], 2), "sel_experts": sel1.reshape(NE1 + 1, 2 * G1, P),
        "bias_fc": bias_fc, "bias_proj": bias_proj.reshape(2 * G1, P),
    }
    arrays = {f"in_{n}": np.ascontiguousarray(v) for n, v in arrays.items()}
    nc = bacc.Bacc("TRN2", target_bir_lowering=False, num_devices=1)
    aps = {n[3:]: nc.dram_tensor(n, v.shape, mybir.dt.from_np(v.dtype), kind="ExternalInput").ap() for n, v in arrays.items()}
    out = nc.dram_tensor("out_xT", (P, TOK), F32, kind="ExternalOutput").ap()
    build(nc, aps, out)
    r = run_bass_kernel_spmd(nc, [arrays], core_ids=[0])
    return r.results[0]["out_xT"].T.reshape(B, S, E)
```

```python
from contextlib import ExitStack

import numpy as np

import concourse.bass as bass
from concourse import mybir

F32 = mybir.dt.float32
F32R = mybir.dt.float32r
BF16 = mybir.dt.bfloat16
ALU = mybir.AluOpType
ACT = mybir.ActivationFunctionType
AX = mybir.AxisListType

B, S, E = 2, 1024, 128
TOK = B * S
P = 128
H, HD = 16, 8
HQ = 4
NQUAD = H // HQ
NIT = B * NQUAD
HP = P // HQ
KB = S // P
GW = 512
NG = TOK // GW
NPART = 3
PAIRS = NPART * NPART * HD
ONES_ROW = 96
EPS = 1e-5
BF16_ONES = float(np.array([0x3F803F80], np.uint32).view(np.float32)[0])

NE0, I0 = 64, 88
NGRP, GSZ, TOPG, TOP0 = 8, 8, 4, 8
ROUTED_SCALE = 2.5
CH0 = NE0 * I0 // P
SHI = 2 * I0
CHS = -(-SHI // P)
DL = 32
DECAY = 0.01
NE1, HID = 8, 512
CH1 = HID // P




class Sems:

    def __init__(self, nc, ctx):
        self.nc, self.ctx = nc, ctx

    def __call__(self, name):
        return self.ctx.enter_context(self.nc.semaphore(name))


def wait(eng, sem, value):
    if not isinstance(value, int) or value > 0:
        eng.wait_ge(sem, value)


def sbuf(nc, ctx):
    return lambda name, shape, dt: ctx.enter_context(nc.sbuf_tensor(name, shape, dt))


def psum(nc, ctx):
    return lambda name, width=GW: ctx.enter_context(nc.psum_tensor(name, [P, width], F32))


def project_l0(nc, X, wq, wk, headsel, QS, KS, QN, KN):
    ROWS = 32
    with ExitStack() as ctx:
        sb, pb, sem = sbuf(nc, ctx), psum(nc, ctx), Sems(nc, ctx)
        Wq, Wk = sb("p0_Wq", [P, P], F32), sb("p0_Wk", [P, P], F32)
        Hs = sb("p0_Hs", [P, ROWS], F32)
        square = sb("p0_square", [P, 2, TOK], F32)
        k2 = sb("p0_k2", [P, TOK], F32)
        rest = sb("p0_rest", [P, 2, TOK], F32)
        part = sb("p0_part", [P, 2, NPART, TOK], BF16)
        nrest = sb("p0_nrest", [2 * ROWS, TOK], F32)
        npart = sb("p0_npart", [2 * ROWS, NPART, TOK], BF16)
        psQ, psK, psN = ([pb(f"p0_{n}{s}") for s in range(2)] for n in ("psQ", "psK", "psN"))
        (loaded, proj_ready, squared, k2_done, norm_ready, part1, rest_done, part2, part3, norm_step, norm3, stored) = (
            sem(f"p0_{n}") for n in ("loaded", "proj_ready", "squared", "k2_done", "norm_ready", "part1", "rest_done",
                                     "part2", "part3", "norm_step", "norm3", "stored"))

        def grp(g):
            return slice(g * GW, (g + 1) * GW)

        with nc.Block() as block:
            @block.sync
            def _(sp):
                sp.dma_start(Wq[:], wq).then_inc(loaded, 16)
                sp.dma_start(Wk[:], wk).then_inc(loaded, 16)
                sp.dma_start(Hs[:], headsel).then_inc(loaded, 16)
                for g in range(NG):
                    for m, (dst, copies) in enumerate(((QS, NPART), (KS, NPART + 2))):
                        for i, written in enumerate((part1, part2, part3)):
                            sp.wait_ge(written, g * 2 + m + 1)
                            for at in range(i, copies, NPART):
                                sp.dma_start(dst[:, at, :, grp(g)], part[:, m, i, grp(g)]).then_inc(stored, 16)
                    sp.wait_ge(norm_step, g * 3 + 3)
                    sp.wait_ge(norm3, g + 1)
                    sp.dma_start(QN[:, :, grp(g)], npart[0:H, :, grp(g)]).then_inc(stored, 16)
                    sp.dma_start(KN[:, :, grp(g)], npart[ROWS:ROWS + H, :, grp(g)]).then_inc(stored, 16)
                sp.wait_ge(stored, NG * (NPART + NPART + 2 + 2) * 16)

            @block.tensor
            def _(pe):
                pe.wait_ge(loaded, 48)

                def project(g):
                    if g >= 2:
                        pe.wait_ge(squared, (g - 1) * 2)
                        pe.wait_ge(part1, (g - 1) * 2)
                        pe.wait_ge(rest_done, (g - 1) * 2)
                    nc.tensor.matmul(psQ[g % 2][:], Wq[:], X[:, grp(g)], start=True, stop=True).then_inc(proj_ready, 1)
                    nc.tensor.matmul(psK[g % 2][:], Wk[:], X[:, grp(g)], start=True, stop=True).then_inc(proj_ready, 1)

                project(0)
                for g in range(NG):
                    if g + 1 < NG:
                        project(g + 1)
                    if g >= 2:
                        pe.wait_ge(norm_step, (g - 2) * 3 + 2)
                    for m in range(2):
                        pe.wait_ge(squared, g * 2 + m + 1)
                        nc.tensor.matmul(psN[g % 2][m * ROWS:(m + 1) * ROWS, :], Hs[:], square[:, m, grp(g)],
                                         start=True, stop=True).then_inc(norm_ready, 1)

            @block.scalar
            def _(act):
                for g in range(NG):
                    for m, ps in enumerate((psQ, psK)):
                        act.wait_ge(proj_ready, g * 2 + m + 1)
                        nc.scalar.activation(part[:, m, 0, grp(g)], ps[g % 2][:], ACT.Copy, scale=(1.0, -2.0)[m]).then_inc(part1, 1)
                        nc.scalar.activation(square[:, m, grp(g)], ps[g % 2][:], ACT.Square).then_inc(squared, 1)
                    for m in range(2):
                        act.wait_ge(rest_done, g * 2 + m + 1)
                        nc.scalar.activation(part[:, m, 1, grp(g)], rest[:, m, grp(g)], ACT.Copy).then_inc(part2, 1)

            @block.vector
            def _(dve):
                for g in range(NG):
                    dve.wait_ge(squared, g * 2 + 1)
                    nc.vector.tensor_tensor(rest[:, 0, grp(g)], psQ[g % 2][:], part[:, 0, 0, grp(g)], ALU.subtract).then_inc(rest_done, 1)
                    dve.wait_ge(squared, g * 2 + 2)
                    nc.vector.tensor_scalar(k2[:, grp(g)], psK[g % 2][:], -2.0, None, ALU.mult).then_inc(k2_done, 1)
                    dve.wait_ge(k2_done, g + 1)
                    nc.vector.tensor_tensor(rest[:, 1, grp(g)], k2[:, grp(g)], part[:, 1, 0, grp(g)], ALU.subtract).then_inc(rest_done, 1)
                    dve.wait_ge(norm_ready, g * 2 + 2)
                    norm = psN[g % 2][0:2 * ROWS, :]
                    nc.vector.tensor_copy(npart[:, 0, grp(g)], norm).then_inc(norm_step, 1)
                    dve.wait_ge(norm_step, g * 3 + 1)
                    nc.vector.tensor_tensor(nrest[:, grp(g)], norm, npart[:, 0, grp(g)], ALU.subtract).then_inc(norm_step, 1)
                    dve.wait_ge(norm_step, g * 3 + 2)
                    nc.vector.tensor_copy(npart[:, 1, grp(g)], nrest[:, grp(g)]).then_inc(norm_step, 1)

            @block.gpsimd
            def _(pool):
                for g in range(NG):
                    for m in range(2):
                        pool.wait_ge(part2, g * 2 + m + 1)
                        nc.gpsimd.tensor_tensor(part[:, m, 2, grp(g)], rest[:, m, grp(g)], part[:, m, 1, grp(g)],
                                                ALU.subtract).then_inc(part3, 1)
                    pool.wait_ge(norm_step, g * 3 + 3)
                    nc.gpsimd.tensor_tensor(npart[:, 2, grp(g)], nrest[:, grp(g)], npart[:, 1, grp(g)], ALU.subtract).then_inc(norm3, 1)


TILES0 = [[(7, 0, 1024)], [(6, 0, 896), (0, 896, 128)], [(5, 0, 768), (1, 768, 256)],
          [(4, 0, 640), (2, 640, 384)], [(3, 0, 512)]]
WIDTH0 = [sum(r[2] for r in t) for t in TILES0]


def pieces(a, b, cut=GW):
    while a < b:
        e = min(b, (a // cut + 1) * cut)
        yield a, e
        a = e


def attention_l0(nc, x_dram, wv, gamma, QS, KS, QN, KN, OALL):
    NT = len(TILES0)
    RING, LAG = 3, 2
    STEPS = 1 + NT * HQ
    LOADS = (3 + 3 + 2 + 2) * 16
    assert STEPS % RING == 0
    with ExitStack() as ctx:
        sb, pb, sem = sbuf(nc, ctx), psum(nc, ctx), Sems(nc, ctx)
        QP = [sb(f"a0_QP{s}", [P, HQ, S], BF16) for s in range(2)]
        KP = [sb(f"a0_KP{s}", [P, HQ, S], BF16) for s in range(2)]
        XB = [sb(f"a0_XB{s}", [P, S], F32) for s in range(2)]
        WV = [sb(f"a0_WV{s}", [P, P], F32) for s in range(2)]
        V = [sb(f"a0_V{s}", [P, S], F32) for s in range(2)]
        PR = [sb(f"a0_PR{T}", [P, HQ, S], F32) for T in range(NT)]
        gam, ng, lo, hi = (sb(f"a0_{n}", [P, H], F32) for n in ("gam", "ng", "lo", "hi"))
        ring = [pb(f"a0_ring{r}", S) for r in range(RING)]
        OUT = pb("a0_OUT", S)
        pack_loaded = [sem(f"pack_loaded{s}") for s in range(2)]
        slot_set = [sem(f"slot_set{s}") for s in range(2)]
        gamma_loaded, gamma_ready = sem("gamma_loaded"), sem("gamma_ready")
        ring_filled, ring_read, clamped, masked, pv_done, out_read = (
            sem(n) for n in ("ring_filled", "ring_read", "clamped", "masked", "pv_done", "out_read"))


        def set_slot(eng, nc_eng, s):
            for n, (rows, value) in enumerate(((QP[s][64:96], 0.0), (QP[s][96:P], BF16_ONES),
                                               (KP[s][64:96], BF16_ONES), (KP[s][96:P], 0.0))):
                if n:
                    eng.wait_ge(slot_set[s], n)
                nc_eng.memset(rows.bitcast(F32), value).then_inc(slot_set[s], 1)
            eng.wait_ge(slot_set[s], 4)

        with nc.Block() as block:
            @block.sync
            def _(sp):
                sp.dma_start(gam[:], gamma.partition_broadcast(P)).then_inc(gamma_loaded, 16)

                def load(b, q, s):
                    tok, heads = bass.ds(b * S, S), bass.ds(q * HQ, HQ)
                    got = pack_loaded[s]
                    for r in range(NPART):
                        rows = slice(r * 24, r * 24 + 24)
                        sp.dma_start(QP[s][rows], QS[heads, :, :, tok].rearrange("h i d t -> (i d) h t")).then_inc(got, 16)
                        sp.dma_start(KP[s][rows], KS[heads, r:r + 3, :, tok].rearrange("h i d t -> (i d) h t")).then_inc(got, 16)
                    sp.dma_start(QP[s][PAIRS:PAIRS + 3], QN[heads, :, tok].rearrange("h i t -> i h t")).then_inc(got, 16)
                    sp.dma_start(KP[s][ONES_ROW:ONES_ROW + 3], KN[heads, :, tok].rearrange("h i t -> i h t")).then_inc(got, 16)
                    sp.dma_start(XB[s][:], x_dram[:, tok]).then_inc(got, 16)
                    sp.dma_start(WV[s][:], wv[bass.ds(q, 1)].rearrange("a e n -> (a e) n")).then_inc(got, 16)

                for s in range(2):
                    sp.wait_ge(slot_set[s], 4)
                    load(0, s, s)
                with sp.Fori(1, NIT // 2) as k:
                    for s in range(2):
                        sp.wait_ge(ring_read, (k * 2 + (s - 1)) * STEPS)
                        sp.nop(nofuse=True)
                        load(k // 2, (k % 2) * 2 + s, s)

            @block.gpsimd
            def _(pool):
                set_slot(pool, nc.gpsimd, 1)

                def mask(it, T, s):
                    for j in range(HQ):
                        pool.wait_ge(clamped, it * (NT * HQ) + (T * HQ + j + 1))
                        pool.nop(nofuse=True)
                        for kb, c0, n in TILES0[T]:
                            d = PR[T][:, j, c0 + n - P:c0 + n]
                            last = nc.gpsimd.affine_select(out=d, in_=d, compare_op=ALU.is_gt, fill=0.0, base=0,
                                                           pattern=[[-1, P]], channel_multiplier=1)
                        last.then_inc(masked, 1)

                with pool.Fori(0, NIT // 2) as k:
                    for s in range(2):
                        for T in range(NT):
                            mask(k * 2 + s, T, s)

            @block.tensor
            def _(pe):
                def values(it, k, s):
                    pe.wait_ge(pack_loaded[s], k * LOADS + LOADS)
                    if not isinstance(it, int) or it > 0:
                        pe.wait_ge(ring_read, it * STEPS - RING + 1)
                    for kb in range(KB):
                        last = nc.tensor.matmul(ring[0][:, kb * P:(kb + 1) * P], XB[s][:, kb * P:(kb + 1) * P],
                                                WV[s][:], start=True, stop=True)
                    last.then_inc(ring_filled, 1)

                def scores(it, T, j, s):
                    n = 1 + T * HQ + j
                    if not isinstance(it, int) or it > 0 or n >= RING:
                        pe.wait_ge(ring_read, it * STEPS + (n - RING + 1))
                    for kb, c0, w in TILES0[T]:
                        for a, b in pieces(c0, c0 + w):
                            last = nc.tensor.matmul(ring[n % RING][:, a:b], KP[s][:, j, kb * P:(kb + 1) * P],
                                                    QP[s][:, j, a - c0:b - c0], start=True, stop=True)
                    last.then_inc(ring_filled, 1)

                def weigh(it, T, s, quarter):
                    if quarter == 0:
                        pe.wait_ge(masked, it * (NT * HQ) + (T + 1) * HQ)
                        if T == 0 and (not isinstance(it, int) or it > 0):
                            pe.wait_ge(out_read, it)
                    done = 0
                    for kb, c0, w in TILES0[T]:
                        for a, b in pieces(0, w, GW // 2):
                            at, done = done, done + b - a
                            if at // (GW // 2) != quarter:
                                continue
                            for j in range(HQ):
                                rows = slice(j * HP, (j + 1) * HP)
                                last = nc.tensor.matmul(OUT[rows, a:b], V[s][:, kb * P + j * HP:kb * P + (j + 1) * HP],
                                                        PR[T][:, j, c0 + a:c0 + b], start=(T == 0 and a % GW == 0),
                                                        stop=(T == NT - 1), skip_group_check=True)
                    if quarter == (WIDTH0[T] - 1) // (GW // 2):
                        last.then_inc(pv_done, 1)

                def pair(it, k, s, last_pair):
                    for T in range(NT):
                        ahead = T + LAG < NT or not last_pair
                        if T + LAG == NT and ahead:
                            values(it + 1, k + s, 1 - s)
                        for j in range(HQ):
                            if T + LAG < NT:
                                scores(it, T + LAG, j, s)
                            elif ahead:
                                scores(it + 1, T + LAG - NT, j, 1 - s)
                            for quarter in {0: (), 1: (), 2: (0, 1), 3: (2, 3)}[j] if T == 0 else (j,):
                                if quarter <= (WIDTH0[T] - 1) // (GW // 2):
                                    weigh(it, T, s, quarter)

                values(0, 0, 0)
                for T in range(LAG):
                    for j in range(HQ):
                        scores(0, T, j, 0)
                pair(0, 0, 0, False)
                pair(1, 0, 1, False)
                with pe.Fori(1, NIT // 2 - 1) as k:
                    for s in range(2):
                        pair(k * 2 + s, k, s, False)
                pair(NIT - 2, NIT // 2 - 1, 0, False)
                pair(NIT - 1, NIT // 2 - 1, 1, True)

            @block.scalar
            def _(act):
                act.wait_ge(gamma_ready, 3)

                def pair(it, b_quad, s, first):
                    act.wait_ge(ring_filled, it * STEPS + 1)
                    if not first:
                        act.wait_ge(pv_done, it * NT - NT)
                    nc.scalar.activation(V[s][:], ring[0][:], ACT.Copy).then_inc(ring_read, 1)
                    for T in range(NT):
                        for j in range(HQ):
                            n = 1 + T * HQ + j
                            act.wait_ge(ring_filled, it * STEPS + (n + 1))
                            if j == 0 and not first:
                                act.wait_ge(pv_done, it * NT + (T + 1 - NT))
                            act.nop(nofuse=True)
                            head = bass.ds(b_quad * HQ + j, 1)
                            nc.scalar.activation(PR[T][:, j, 0:WIDTH0[T]], ring[n % RING][:, 0:WIDTH0[T]],
                                                 ACT.Exp, scale=ng[:, head]).then_inc(ring_read, 1)

                pair(0, 0, 0, True)
                pair(1, 1, 1, False)
                with act.Fori(1, NIT // 2) as k:
                    for s in range(2):
                        pair(k * 2 + s, (k % 2) * 2 + s, s, False)

            @block.vector
            def _(dve):
                set_slot(dve, nc.vector, 0)
                dve.wait_ge(gamma_loaded, 16)
                nc.vector.tensor_scalar(ng[:], gam[:], -1.0 / float(np.sqrt(HD)), None, ALU.mult).then_inc(gamma_ready, 1)
                nc.vector.tensor_scalar(lo[:], gam[:], 0.0, None, ALU.is_lt).then_inc(gamma_ready, 1)
                dve.wait_ge(gamma_ready, 2)
                nc.vector.tensor_scalar(hi[:], lo[:], 3.0e38, 1.0, ALU.mult, ALU.add).then_inc(gamma_ready, 1)
                dve.wait_ge(gamma_ready, 3)

                def clamp(it, T, s, b_quad):
                    for j in range(HQ):
                        dve.wait_ge(ring_read, it * STEPS + (2 + T * HQ + j))
                        p = PR[T][:, j, 0:WIDTH0[T]]
                        head = bass.ds(b_quad * HQ + j, 1)
                        nc.vector.tensor_scalar(p, p, lo[:, head], hi[:, head], ALU.max, ALU.min).then_inc(clamped, 1)

                def copy_out(it):
                    dve.wait_ge(pv_done, it * NT + NT)
                    o = OALL[:, bass.ds(it, 1), :] if not isinstance(it, int) else OALL[:, it, :]
                    nc.vector.tensor_copy(o, OUT[:]).then_inc(out_read, 1)

                def pair(it, b_quad, s, first):
                    for T in range(NT):
                        clamp(it, T, s, b_quad)
                        if T == 1 and not first:
                            copy_out(it - 1)

                pair(0, 0, 0, True)
                pair(1, 1, 1, False)
                with dve.Fori(1, NIT // 2) as k:
                    for s in range(2):
                        pair(k * 2 + s, (k % 2) * 2 + s, s, False)
                copy_out(NIT - 1)


def add_and_norm(nc, name, X, Y, consts, terms=None, loads=(), out=None):
    mean_of = consts["mean_of"]
    TG = GW // P
    with ExitStack() as ctx:
        sb, pb, sem = sbuf(nc, ctx), psum(nc, ctx), Sems(nc, ctx)
        C = [sb(f"{name}_C{g}", [P, GW], F32) for g in range(NG)]
        Q = [sb(f"{name}_Q{g}", [P, GW], F32) for g in range(NG)]
        dev_of = sb(f"{name}_dev_of", [P, NG, TG], F32)
        inv_of = sb(f"{name}_inv_of", [P, NG, TG], F32)
        first = [pb(f"{name}_mean{g}") for g in range(NG)]
        scale = [pb(f"{name}_scale{g}") for g in range(NG)]
        mean, centred, squared, variance, dev, inv, spread, done = (
            sem(f"{name}_{n}") for n in ("mean", "centred", "squared", "variance", "dev", "inv", "spread", "done"))
        if terms:
            loaded, delta, y_ready = (sem(f"{name}_{n}") for n in ("loaded", "delta", "y_ready"))
        if out is not None:
            stored = sem(f"{name}_stored")

        def grp(t, g):
            return t[:, g * GW:(g + 1) * GW]

        with nc.Block() as block:
            @block.sync
            def _(sp):
                for tile, src in loads:
                    sp.dma_start(tile, src).then_inc(loaded, 16)
                if out is not None:
                    for g in range(NG):
                        sp.wait_ge(done, g + 1)
                        sp.dma_start(grp(out, g), grp(X, g)).then_inc(stored, 16)
                    sp.wait_ge(stored, 16 * NG)

            @block.tensor
            def _(pe):
                def spread_inverse(g):
                    pe.wait_ge(inv, g + 1)
                    for t in range(TG):
                        last = nc.tensor.matmul(scale[g][:, t * P:(t + 1) * P], inv_of[:, g, t:t + 1].to_broadcast([P, P]),
                                                consts["ident"][:], start=True, stop=True)
                    last.then_inc(spread, 1)

                if terms:
                    pe.wait_ge(loaded, 16 * len(loads))
                    for g in range(NG):
                        pairs = terms(g)
                        for n, (a, b) in enumerate(pairs):
                            last = nc.tensor.matmul(first[g][:], a, b, start=(n == 0), stop=(n == len(pairs) - 1))
                        last.then_inc(delta, 1)
                for g in range(NG):
                    if terms:
                        pe.wait_ge(y_ready, g + 1)
                    nc.tensor.matmul(first[g][:], mean_of[:], grp(Y, g), start=True, stop=True).then_inc(mean, 1)
                for g in range(NG):
                    pe.wait_ge(squared, g + 1)
                    for t in range(TG):
                        last = nc.tensor.matmul(scale[g][:, t:t + 1], Q[g][:, t * P:(t + 1) * P], mean_of[:, 0:1],
                                                start=True, stop=True)
                    last.then_inc(variance, 1)
                    if g:
                        spread_inverse(g - 1)
                spread_inverse(NG - 1)

            @block.vector
            def _(dve):
                if terms:
                    for g in range(NG):
                        dve.wait_ge(delta, g + 1)
                        nc.vector.tensor_tensor(grp(Y, g), grp(X, g), first[g][:], ALU.add).then_inc(y_ready, 1)
                    dve.wait_ge(y_ready, NG)

                def centre(g):
                    dve.wait_ge(mean, g + 1)
                    nc.vector.tensor_tensor(C[g][:], grp(Y, g), first[g][:], ALU.subtract).then_inc(centred, 1)

                def invert(g):
                    dve.wait_ge(dev, g + 1)
                    nc.vector.reciprocal(inv_of[:, g], dev_of[:, g]).then_inc(inv, 1)

                centre(0)
                centre(1)
                for g in range(NG):
                    invert(g)
                    if g + 2 < NG:
                        centre(g + 2)
                    dve.wait_ge(spread, g + 1)
                    nc.vector.tensor_tensor(grp(X, g), C[g][:], scale[g][:], ALU.mult).then_inc(done, 1)
                dve.wait_ge(done, NG)

            @block.scalar
            def _(act):
                def square(g):
                    act.wait_ge(centred, g + 1)
                    nc.scalar.activation(Q[g][:], C[g][:], ACT.Square).then_inc(squared, 1)

                square(0)
                for g in range(NG):
                    if g + 1 < NG and g < 1:
                        square(g + 1)
                    act.wait_ge(variance, g + 1)
                    nc.scalar.activation(dev_of[:, g], scale[g][:, 0:TG], ACT.Sqrt, bias=consts["eps"][:]).then_inc(dev, 1)
                    if g + 2 < NG:
                        square(g + 2)


NT_TOK = TOK // P




def route_l0(nc, X, gate_w, gate_bias, earlier, consts, GT):
    with ExitStack() as ctx:
        sb, pb, sem = sbuf(nc, ctx), psum(nc, ctx), Sems(nc, ctx)
        W = sb("r0_W", [P, NE0], F32)
        bias = sb("r0_bias", [P, NE0], F32)
        tri = sb("r0_tri", [P, NGRP, NGRP], F32)
        sc = sb("r0_scores", [P, NT_TOK, NE0], F32)
        ch = sb("r0_choice", [P, NT_TOK, NE0], F32)
        t1 = sb("r0_t1", [P, NT_TOK, NE0], F32)
        t2 = sb("r0_t2", [P, NT_TOK, NE0], F32)
        m1, m2, cnt = (sb(f"r0_{n}", [P, NT_TOK * NGRP], F32) for n in ("m1", "m2", "cnt"))
        top = sb("r0_top", [P, NT_TOK, 8], F32)
        den = sb("r0_den", [P, NT_TOK], F32)
        rw = sb("r0_rw", [P, NT_TOK, 2, NE0], F32)
        psL = pb("r0_psL", NT_TOK * NE0)
        psT = [pb(f"r0_psT{g}") for g in range(NG)]
        loaded, logits, scored, step, turned, copied = (
            sem(f"r0_{n}") for n in ("loaded", "logits", "scored", "step", "turned", "copied"))
        with nc.Block() as block:
            @block.sync
            def _(sp):
                sp.dma_start(W[:], gate_w).then_inc(loaded, 16)
                sp.dma_start(bias[:], gate_bias.partition_broadcast(P)).then_inc(loaded, 16)
                sp.dma_start(tri[:], earlier.partition_broadcast(P)).then_inc(loaded, 16)

            @block.tensor
            def _(pe):
                pe.wait_ge(loaded, 48)
                for t in range(NT_TOK):
                    last = nc.tensor.matmul(psL[:, t * NE0:(t + 1) * NE0], X[:, t * P:(t + 1) * P], W[:],
                                            start=True, stop=True)
                last.then_inc(logits, 1)
                pe.wait_ge(copied, 2)
                for t in range(NT_TOK):
                    last = nc.tensor.transpose(psT[t // 4][:, (t % 4) * P:(t % 4 + 1) * P],
                                               rw[:, t].rearrange("p a e -> p (a e)"), consts["ident"][:])
                    if t % 4 == 3:
                        last.then_inc(turned, 1)

            @block.scalar
            def _(act):
                act.wait_ge(logits, 1)
                nc.scalar.activation(sc[:].rearrange("p t e -> p (t e)"), psL[:], ACT.Sigmoid).then_inc(scored, 1)

            @block.vector
            def _(dve):
                n = [0]

                def link(ins):
                    n[0] += 1
                    ins.then_inc(step, 1)
                    dve.wait_ge(step, n[0])

                v = nc.vector
                byg = lambda t: t[:].rearrange("p t (g e) -> p (t g) e", g=NGRP)
                wide = lambda t, k: t.unsqueeze(2).to_broadcast([P, NT_TOK * NGRP, k])
                dve.wait_ge(loaded, 48)
                dve.wait_ge(scored, 1)
                link(v.tensor_tensor(ch[:], sc[:], bias[:].unsqueeze(1).to_broadcast([P, NT_TOK, NE0]), ALU.add))
                link(v.tensor_reduce(m1[:], byg(ch), AX.X, ALU.max))
                link(v.tensor_tensor(byg(t1), byg(ch), wide(m1[:], GSZ), ALU.is_equal))
                link(v.scalar_tensor_tensor(t2[:], t1[:], -1e30, ch[:], ALU.mult, ALU.add))
                link(v.tensor_reduce(m2[:], byg(t2), AX.X, ALU.max))
                link(v.tensor_reduce(cnt[:], byg(t1), AX.X, ALU.add))
                link(v.tensor_scalar(cnt[:], cnt[:], 2.0, -1e30, ALU.is_lt, ALU.mult))
                link(v.tensor_tensor(cnt[:], cnt[:], m1[:], ALU.add))
                link(v.tensor_tensor(m2[:], m2[:], cnt[:], ALU.max))
                link(v.tensor_tensor(m1[:], m1[:], m2[:], ALU.add))
                gs = m1[:].rearrange("p (t g) -> p t g", g=NGRP)
                other = gs.unsqueeze(2).to_broadcast([P, NT_TOK, NGRP, NGRP])
                own = gs.unsqueeze(3).to_broadcast([P, NT_TOK, NGRP, NGRP])
                pair = lambda t: t[:].rearrange("p t (i j) -> p t i j", i=NGRP)
                link(v.tensor_tensor(pair(t1), other, own, ALU.is_gt))
                link(v.tensor_tensor(pair(t2), other, own, ALU.is_equal))
                link(v.tensor_tensor(t2[:], t2[:], tri[:].rearrange("p i j -> p (i j)").unsqueeze(1)
                                     .to_broadcast([P, NT_TOK, NE0]), ALU.mult))
                link(v.tensor_tensor(t1[:], t1[:], t2[:], ALU.add))
                link(v.tensor_reduce(cnt[:], byg(t1), AX.X, ALU.add))
                link(v.tensor_scalar(cnt[:], cnt[:], float(TOPG), None, ALU.is_lt))
                link(v.tensor_tensor(byg(t1), byg(ch), wide(cnt[:], GSZ), ALU.mult))
                for t in range(NT_TOK):
                    link(v.max(top[:, t], t1[:, t]))
                    link(v.match_replace(t2[:, t], top[:, t], t1[:, t], 1e30))
                link(v.tensor_scalar(t2[:], t2[:], 1e29, None, ALU.is_ge))
                link(v.tensor_tensor(t1[:], t2[:], sc[:], ALU.mult))
                link(v.tensor_reduce(den[:], t1[:], AX.X, ALU.add))
                link(v.tensor_scalar(den[:], den[:], 1e-20, None, ALU.add))
                link(v.reciprocal(den[:], den[:]))
                link(v.tensor_scalar(den[:], den[:], ROUTED_SCALE, None, ALU.mult))
                for a in range(2):
                    v.tensor_tensor(rw[:, :, a, :], t1[:], den[:].unsqueeze(2).to_broadcast([P, NT_TOK, NE0]),
                                    ALU.mult).then_inc(copied, 1)
                for g in range(NG):
                    dve.wait_ge(turned, g + 1)
                    cols = slice(g * GW, (g + 1) * GW)
                    link(v.tensor_copy(GT[:, cols], psT[g][:]))
                    link(v.tensor_tensor(GT[NE0:P, cols], psT[g][NE0:P, :], GT[NE0:P, cols].bitcast(F32), ALU.subtract))


def experts_l0(nc, X, Y, GT, w_chunks, sel_chunks):
    with ExitStack() as ctx:
        sb, pb, sem = sbuf(nc, ctx), psum(nc, ctx), Sems(nc, ctx)
        XH, XL = sb("e0_XH", [P, TOK], F32R), sb("e0_XL", [P, TOK], F32R)
        RAW = [sb(f"e0_RAW{s}", [P, 3, P], F32) for s in range(2)]
        WH = [sb(f"e0_WH{s}", [P, 3, P], F32R) for s in range(2)]
        WL = [sb(f"e0_WL{s}", [P, 3, P], F32R) for s in range(2)]
        SELF = [sb(f"e0_SELF{s}", [P, P], F32) for s in range(2)]
        SEL = [sb(f"e0_SEL{s}", [P, P], F32R) for s in range(2)]
        SG = [sb(f"e0_SG{s}", [P, GW], F32) for s in range(2)]
        T = [sb(f"e0_T{s}", [P, GW], F32) for s in range(2)]
        HT = [sb(f"e0_H{s}", [P, GW], F32) for s in range(4)]
        HH = [sb(f"e0_HH{s}", [P, GW], F32R) for s in range(2)]
        HL = [sb(f"e0_HL{s}", [P, GW], F32R) for s in range(2)]
        acc = [pb(f"e0_acc{g}") for g in range(NG)]
        psG = [pb(f"e0_psG{s}") for s in range(2)]
        psU, psR = pb("e0_psU"), pb("e0_psR")
        x_split = sem("x_split")
        w_loaded = [sem(f"w_loaded{s}") for s in range(2)]
        w_split = [sem(f"w_split{s}") for s in range(2)]
        gate_ready, up_ready, weight_ready, silu_done, mul_done, h_ready, high_done, low_done, down_done, y_done = (
            sem(n) for n in ("gate_ready", "up_ready", "weight_ready", "silu_done", "mul_done", "h_ready",
                             "high_done", "low_done", "down_done", "y_done"))
        LAG = 2
        NSH = CHS * NG
        NCH = CHS + CH0
        with nc.Block() as block:
            @block.sync
            def _(sp):
                def load(c, s):
                    sp.dma_start(RAW[s][:], w_chunks[bass.ds(c, 1)].rearrange("a p k n -> (a p) k n")).then_inc(w_loaded[s], 16)
                    sp.dma_start(SELF[s][:], sel_chunks[bass.ds(c, 1)].rearrange("a p n -> (a p) n")).then_inc(w_loaded[s], 16)
                load(0, 0)
                load(1, 1)
                with sp.Fori(1, NCH // 2) as k:
                    for s in range(2):
                        sp.wait_ge(w_split[s], k * 3)
                        sp.nop(nofuse=True)
                        load(k * 2 + s, s)

            @block.gpsimd
            def _(pool):
                def split(k, s):
                    pool.wait_ge(w_loaded[s], k * 32 + 32)
                    if not isinstance(k, int):
                        pool.wait_ge(down_done, (k * 2 + (s - 1)) * NG)
                    pool.nop(nofuse=True)
                    nc.gpsimd.tensor_copy(WH[s][:], RAW[s][:]).then_inc(w_split[s], 1)
                    nc.gpsimd.tensor_copy(SEL[s][:], SELF[s][:]).then_inc(w_split[s], 1)
                    pool.wait_ge(w_split[s], k * 3 + 2)
                    nc.gpsimd.tensor_tensor(WL[s][:], RAW[s][:], WH[s][:].bitcast(F32), ALU.subtract).then_inc(w_split[s], 1)

                for s in range(2):
                    split(0, s)
                with pool.Fori(1, NCH // 2) as k:
                    for s in range(2):
                        split(k, s)

            @block.tensor
            def _(pe):
                def product(ps, s, i, cols):
                    nc.tensor.matmul(ps[:], WH[s][:, i, :], XH[:, cols], start=True, stop=False)
                    nc.tensor.matmul(ps[:], WH[s][:, i, :], XL[:, cols], start=False, stop=False)
                    return nc.tensor.matmul(ps[:], WL[s][:, i, :], XH[:, cols], start=False, stop=True)

                def down(n, s, g, start=False):
                    pe.wait_ge(low_done, n + 1)
                    for i, (w, h) in enumerate(((WH, HH), (WL, HH), (WH, HL))):
                        last = nc.tensor.matmul(acc[g][:], w[s][:, 2, :], h[g % 2][:], start=(start and i == 0), stop=True,
                                                skip_group_check=True)
                    last.then_inc(down_done, 1)

                def chunk(k, s, shared):
                    pe.wait_ge(w_split[s], k * 3 + 3)
                    for g in range(NG):
                        n = (k * 2 + s) * NG + g
                        peeled = isinstance(k, int)
                        cols = slice(g * GW, (g + 1) * GW)
                        if not (peeled and n < 2):
                            pe.wait_ge(silu_done, n - 1)
                        product(psG[g % 2], s, 0, cols).then_inc(gate_ready, 1)
                        if not (peeled and n < 1):
                            pe.wait_ge(mul_done, n)
                        product(psU, s, 1, cols).then_inc(up_ready, 1)
                        if not shared:
                            pe.wait_ge(h_ready, n)
                            nc.tensor.matmul(psR[:], SEL[s][:], GT[:, cols], start=True, stop=True).then_inc(weight_ready, 1)
                        if not (peeled and n < LAG):
                            if g >= LAG:
                                down(n - LAG, s, g - LAG, start=(shared and s == 0))
                            else:
                                down(n - LAG, 1 - s, g - LAG + NG, start=(shared and s == 1))

                pe.wait_ge(x_split, 2)
                chunk(0, 0, True)
                chunk(0, 1, True)
                with pe.Fori(1, NCH // 2) as k:
                    chunk(k, 0, False)
                    chunk(k, 1, False)
                for n in range(NCH * NG - LAG, NCH * NG):
                    down(n, 1, n % NG)

            @block.scalar
            def _(act):
                def silu(n, g, free):
                    act.wait_ge(gate_ready, n + 1)
                    if free:
                        act.wait_ge(mul_done, n - 1)
                    nc.scalar.activation(SG[g % 2][:], psG[g % 2][:], ACT.Silu).then_inc(silu_done, 1)

                def high(n, g, free):
                    act.wait_ge(h_ready, n + 1)
                    if free:
                        act.wait_ge(down_done, n - 1)
                    nc.scalar.activation(HH[g % 2][:], HT[g % 4][:], ACT.Copy).then_inc(high_done, 1)

                for n in range(NSH):
                    silu(n, n % NG, n >= 2)
                    if n:
                        high(n - 1, (n - 1) % NG, n - 1 >= 2)
                with act.Fori(1, NCH // 2) as k:
                    for i in range(2 * NG):
                        silu(k * (2 * NG) + i, i % NG, True)
                        high(k * (2 * NG) + (i - 1), (i - 1) % NG, True)
                high(NCH * NG - 1, NG - 1, True)

            @block.vector
            def _(dve):
                nc.vector.tensor_copy(XH[:], X[:]).then_inc(x_split, 1)
                dve.wait_ge(x_split, 1)
                nc.vector.tensor_tensor(XL[:], X[:], XH[:].bitcast(F32), ALU.subtract).then_inc(x_split, 1)

                def low(n, g):
                    dve.wait_ge(high_done, n + 1)
                    nc.vector.tensor_tensor(HL[g % 2][:], HT[g % 4][:], HH[g % 2][:].bitcast(F32), ALU.subtract).then_inc(low_done, 1)

                def hidden(n, g, shared, first=False, free=True):
                    dve.wait_ge(up_ready, n + 1)
                    dve.wait_ge(silu_done, n + 1)
                    nc.vector.tensor_tensor(T[g % 2][:], SG[g % 2][:], psU[:], ALU.mult).then_inc(mul_done, 1)
                    if not first:
                        low(n - 1, (g - 1) % NG)
                    dve.wait_ge(mul_done, n + 1)
                    if free:
                        dve.wait_ge(low_done, n - 3)
                    if shared:
                        nc.vector.tensor_copy(HT[g % 4][:], T[g % 2][:]).then_inc(h_ready, 1)
                    else:
                        dve.wait_ge(weight_ready, n - (NSH - 1))
                        nc.vector.tensor_tensor(HT[g % 4][:], T[g % 2][:], psR[:], ALU.mult).then_inc(h_ready, 1)

                for n in range(NSH):
                    hidden(n, n % NG, True, n == 0, n >= 4)
                with dve.Fori(1, NCH // 2) as k:
                    for i in range(2 * NG):
                        hidden(k * (2 * NG) + i, i % NG, False)
                low(NCH * NG - 1, NG - 1)
                dve.wait_ge(down_done, NCH * NG)
                for g in range(NG):
                    cols = slice(g * GW, (g + 1) * GW)
                    nc.vector.tensor_tensor(Y[:, cols], X[:, cols], acc[g][:], ALU.add).then_inc(y_done, 1)
                dve.wait_ge(y_done, NG)


def project_l1(nc, X, weights, decays, QS, KS, LATD):
    NV = 4
    STORES = (3, 3, 5, 5)
    with ExitStack() as ctx:
        sb, pb, sem = sbuf(nc, ctx), psum(nc, ctx), Sems(nc, ctx)
        W = {n: sb(f"p1_{n}", list(w.shape), F32) for n, w in weights.items()}
        DEC = sb("p1_DEC", [P, NV, S], F32)
        kv, lat = sb("p1_kv", [P, TOK], F32), sb("p1_lat", [DL, TOK], F32)
        val, rest = sb("p1_val", [P, NV, TOK], F32), sb("p1_rest", [P, NV, TOK], F32)
        part = sb("p1_part", [P, NV, NPART, TOK], BF16)
        psQ, psKV, psL, psK = ([pb(f"p1_{n}{s}") for s in range(2)] for n in ("psQ", "psKV", "psL", "psK"))
        loaded, dec_loaded, q_ready, kv_ready, kv_read, lat_ready, lat_read, k_ready, val_done, rest_done, part1, part2, part3, stored = (
            sem(f"p1_{n}") for n in ("loaded", "dec_loaded", "q_ready", "kv_ready", "kv_read", "lat_ready", "lat_read", "k_ready",
                                     "val_done", "rest_done", "part1", "part2", "part3", "stored"))

        def grp(g):
            return slice(g * GW, (g + 1) * GW)

        with nc.Block() as block:
            @block.sync
            def _(sp):
                for n, w in weights.items():
                    sp.dma_start(W[n][:], w).then_inc(loaded, 16)
                sp.dma_start(DEC[:], decays.partition_broadcast(P)).then_inc(dec_loaded, 16)
                for g in range(NG):
                    sp.wait_ge(lat_read, g + 1)
                    sp.dma_start(LATD[:, grp(g)], lat[:, grp(g)]).then_inc(stored, 16)
                    for w in range(NV):
                        dst = (QS if w < 2 else KS)[w % 2]
                        for i, written in enumerate((part1, part2, part3)):
                            sp.wait_ge(written, g * NV + w + 1)
                            for at in range(i, STORES[w], NPART):
                                sp.dma_start(dst[:, at, :, grp(g)], part[:, w, i, grp(g)]).then_inc(stored, 16)
                sp.wait_ge(stored, NG * (1 + sum(STORES)) * 16)

            @block.tensor
            def _(pe):
                pe.wait_ge(loaded, 16 * len(weights))

                def first(g):
                    xg = X[:, grp(g)]
                    if g >= 2:
                        pe.wait_ge(kv_read, g - 1)
                    nc.tensor.matmul(psKV[g % 2][:], W["wk"][:], xg, start=True, stop=False)
                    nc.tensor.matmul(psKV[g % 2][:], W["wv"][:], xg, start=False, stop=True).then_inc(kv_ready, 1)
                    if g >= 2:
                        pe.wait_ge(val_done, (g - 2) * NV + 2)
                    nc.tensor.matmul(psQ[g % 2][:], W["wq"][:], xg, start=True, stop=True).then_inc(q_ready, 1)

                first(0)
                for g in range(NG):
                    if g + 1 < NG:
                        first(g + 1)
                    pe.wait_ge(kv_read, g + 1)
                    if g >= 2:
                        pe.wait_ge(lat_read, g - 1)
                    nc.tensor.matmul(psL[g % 2][0:DL, :], W["down"][:], kv[:, grp(g)], start=True, stop=True).then_inc(lat_ready, 1)
                    pe.wait_ge(lat_read, g + 1)
                    if g >= 2:
                        pe.wait_ge(val_done, (g - 1) * NV)
                    nc.tensor.matmul(psK[g % 2][:], W["upk"][:], lat[:, grp(g)], start=True, stop=True).then_inc(k_ready, 1)

            @block.scalar
            def _(act):
                def copy_kv(g):
                    act.wait_ge(kv_ready, g + 1)
                    nc.scalar.activation(kv[:, grp(g)], psKV[g % 2][:], ACT.Copy).then_inc(kv_read, 1)

                def copy_lat(g):
                    act.wait_ge(lat_ready, g + 1)
                    nc.scalar.activation(lat[:, grp(g)], psL[g % 2][0:DL, :], ACT.Copy).then_inc(lat_read, 1)

                def first_part(g, w):
                    act.wait_ge(val_done, g * NV + w + 1)
                    nc.scalar.activation(part[:, w, 0, grp(g)], val[:, w, grp(g)], ACT.Copy).then_inc(part1, 1)

                def second_part(g, w):
                    act.wait_ge(rest_done, g * NV + w + 1)
                    nc.scalar.activation(part[:, w, 1, grp(g)], rest[:, w, grp(g)], ACT.Copy).then_inc(part2, 1)

                copy_kv(0)
                for g in range(NG):
                    if g == 0:
                        first_part(g, 0)
                        copy_lat(g)
                    else:
                        first_part(g, 0)
                    if g + 1 < NG:
                        copy_kv(g + 1)
                    first_part(g, 1)
                    second_part(g, 0)
                    first_part(g, 2)
                    if g + 1 < NG:
                        copy_lat(g + 1)
                    second_part(g, 1)
                    first_part(g, 3)
                    second_part(g, 2)
                    second_part(g, 3)

            @block.vector
            def _(dve):
                dve.wait_ge(dec_loaded, 16)
                for g in range(NG):
                    pos = slice((g % 2) * GW, (g % 2 + 1) * GW)
                    for w in range(NV + 1):
                        if w < NV:
                            if w % 2 == 0:
                                dve.wait_ge(k_ready if w else q_ready, g + 1)
                            src = (psQ if w < 2 else psK)[g % 2]
                            nc.vector.tensor_tensor(val[:, w, grp(g)], src[:], DEC[:, w, pos], ALU.mult).then_inc(val_done, 1)
                        if w:
                            dve.wait_ge(part1, g * NV + w)
                            nc.vector.tensor_tensor(rest[:, w - 1, grp(g)], val[:, w - 1, grp(g)], part[:, w - 1, 0, grp(g)],
                                                    ALU.subtract).then_inc(rest_done, 1)

            @block.gpsimd
            def _(pool):
                for g in range(NG):
                    for w in range(NV):
                        pool.wait_ge(part2, g * NV + w + 1)
                        nc.gpsimd.tensor_tensor(part[:, w, 2, grp(g)], rest[:, w, grp(g)], part[:, w, 1, grp(g)],
                                                ALU.subtract).then_inc(part3, 1)


SLOTS1 = 3


def attention_l1(nc, upv, correct, ident16, QS, KS, LATD, OD):
    NT = KB + 1
    LAG = 2
    NS = NT * HQ * 2
    NM = KB * HQ * 2
    MS = NM + 4
    EARLY = 20
    LOADS = (6 + 6 + 2) * 16
    assert NS % 3 == 0 and SLOTS1 * MS % 3 == 0
    with ExitStack() as ctx:
        sb, pb, sem = sbuf(nc, ctx), psum(nc, ctx), Sems(nc, ctx)
        QP = [sb(f"a1_QP{s}", [P, 2, HQ, S], BF16) for s in range(SLOTS1)]
        KP = [sb(f"a1_KP{s}", [P, 2, HQ, S], BF16) for s in range(SLOTS1)]
        LAT = [sb(f"a1_LAT{s}", [DL, S], F32) for s in range(SLOTS1)]
        WV = [sb(f"a1_WV{s}", [DL, P], F32) for s in range(SLOTS1)]
        V = [sb(f"a1_V{s}", [P, S], F32) for s in range(SLOTS1)]
        PR = [sb(f"a1_PR{r}", [P, HQ, S], F32) for r in range(3)]
        COR = sb("a1_COR", [P, 896], F32)
        junk = sb("a1_junk", [P, 2, GW], BF16)
        OST = sb("a1_OST", [P, S], F32)
        half_max = sb("a1_half_max", [P, HQ, KB, 2], F32)
        neg = sb("a1_neg", [P, HQ * KB], F32)
        neg_part = sb("a1_neg_part", [P, 2, HQ * KB], BF16)
        ID = sb("a1_ID", [P, P], BF16)
        MT = sb("a1_MT", [HQ * KB, 2, P], BF16)
        ring = [pb(f"a1_ring{r}") for r in range(3)]
        mring = [pb(f"a1_mring{r}") for r in range(3)]
        OUT = pb("a1_OUT", S)
        slot_set = [sem(f"slot_set{s}") for s in range(SLOTS1)]
        pack_loaded = [sem(f"pack_loaded{s}") for s in range(SLOTS1)]
        (cor_loaded, s_filled, s_read, m_filled, m_read, masked, pv_done, out_read, out_stored, neg_done, m_rows,
         v_set) = (sem(n) for n in ("cor_loaded", "s_filled", "s_read", "m_filled", "m_read", "masked", "pv_done",
                                    "out_read", "out_stored", "neg_done", "m_rows", "v_set"))

        def known(it):
            return isinstance(it, int)

        def score_cols(T):
            for a, b in pieces(0, T * P):
                yield a, b, T - 1, 0
            for a, b in pieces(T * P, S):
                yield a, b, T, 1

        def set_slot(eng, nc_eng, s):
            for n, (rows, value) in enumerate(((QP[s][64:96], 0.0), (QP[s][96:P], 0.0), (KP[s][64:96], BF16_ONES),
                                               (KP[s][96:P], 0.0))):
                if n:
                    eng.wait_ge(slot_set[s], n)
                nc_eng.memset(rows.bitcast(F32), value).then_inc(slot_set[s], 1)
            eng.wait_ge(slot_set[s], 4)

        with nc.Block() as block:
            @block.sync
            def _(sp):
                def load(b, q, s):
                    tok, heads = bass.ds(b * S, S), bass.ds(q * HQ, HQ)
                    got = pack_loaded[s]
                    for a in range(2):
                        for r in range(NPART):
                            rows = slice(r * 24, r * 24 + 24)
                            sp.dma_start(QP[s][rows, a], QS[a, heads, :, :, tok].rearrange("h i d t -> (i d) h t")).then_inc(got, 16)
                            sp.dma_start(KP[s][rows, a], KS[a, heads, r:r + 3, :, tok].rearrange("h i d t -> (i d) h t")).then_inc(got, 16)
                    sp.dma_start(LAT[s][:], LATD[:, tok]).then_inc(got, 16)
                    sp.dma_start(WV[s][:], upv[bass.ds(q, 1)].rearrange("a e n -> (a e) n")).then_inc(got, 16)

                def max_rows(it, s):
                    sp.wait_ge(m_read, it * MS + NM + 2)
                    for i in range(2):
                        for a in range(2):
                            sp.dma_start(QP[s][PAIRS + i:PAIRS + i + 1, a], MT[:, i, :]).then_inc(m_rows, 16)

                def store(it):
                    sp.wait_ge(out_read, it + 1)
                    sp.dma_start(OD[bass.ds(it, 1)].rearrange("a p t -> (a p) t"), OST[:]).then_inc(out_stored, 16)

                sp.dma_start(COR[:], correct).then_inc(cor_loaded, 16)
                sp.dma_start(ID[:], ident16).then_inc(cor_loaded, 16)
                for s in range(SLOTS1):
                    sp.wait_ge(slot_set[s], 4)
                    load(0, s, s)
                max_rows(0, 0)
                max_rows(1, 1)

                def refill(it, b, q, s):
                    sp.wait_ge(s_read, it * NS + NS)
                    load(b, q, s)

                refill(0, 0, 3, 0)
                for it in range(1, NIT):
                    store(it - 1)
                    if it + 1 < NIT:
                        max_rows(it + 1, (it + 1) % SLOTS1)
                    if it + 3 <= NIT:
                        refill(it, (it + 3) % NIT // NQUAD, (it + 3) % NQUAD, it % SLOTS1)
                store(NIT - 1)
                sp.wait_ge(out_stored, NIT * 16)

            @block.gpsimd
            def _(pool):
                set_slot(pool, nc.gpsimd, 1)

                with pool.Fori(0, NIT) as it:
                    for T in range(NT):
                        for j in range(HQ):
                            pool.wait_ge(s_read, it * NS + (T * HQ + j + 1) * 2)
                            pool.nop(nofuse=True)
                            if T:
                                d = PR[T % 3][:, j, (T - 1) * P:T * P]
                                last = nc.gpsimd.affine_select(out=d, in_=d, compare_op=ALU.is_ge, fill=0.0, base=0,
                                                               pattern=[[-1, P]], channel_multiplier=1)
                            if T < KB:
                                d = PR[T % 3][:, j, T * P:(T + 1) * P]
                                last = nc.gpsimd.affine_select(out=d, in_=d, compare_op=ALU.is_gt, fill=0.0, base=0,
                                                               pattern=[[1, P]], channel_multiplier=-1)
                            last.then_inc(masked, 1)

            @block.tensor
            def _(pe):
                def ring_free(it, i):
                    if not known(it) or it * MS + i >= 3:
                        pe.wait_ge(m_read, it * MS + (i - 2))

                def max_scores(it, i, s):
                    sb_, j, half = i // (2 * HQ), (i // 2) % HQ, i % 2
                    ring_free(it, i)
                    t0 = half * GW
                    split = min(max((sb_ + 1) * P, t0), t0 + GW)
                    for a, b, var in ((t0, split, 1), (split, t0 + GW, 0)):
                        if a < b:
                            last = nc.tensor.matmul(mring[(s * MS + i) % 3][:, a - t0:b - t0],
                                                    QP[s][0:PAIRS, var, j, sb_ * P:(sb_ + 1) * P],
                                                    KP[s][0:PAIRS, var, j, a:b], start=True, stop=True)
                    last.then_inc(m_filled, 1)

                def turn_max(it, i, s):
                    part = i - NM
                    if part == 0:
                        pe.wait_ge(neg_done, it * 4 + 4)
                    ring_free(it, i)
                    nc.tensor.transpose(mring[(s * MS + i) % 3][0:HQ * KB, 0:P // 2].bitcast(BF16), neg_part[:, part, :], ID[:]).then_inc(m_filled, 1)

                def values(it, i, s):
                    ring_free(it, i)
                    half = i - NM - 2
                    for n in range(4):
                        kb = half * 4 + n
                        last = nc.tensor.matmul(mring[(s * MS + i) % 3][:, n * P:(n + 1) * P], LAT[s][:, kb * P:(kb + 1) * P], WV[s][:],
                                                start=True, stop=True)
                    last.then_inc(m_filled, 1)

                def scores(it, T, j, half, s):
                    n = (T * HQ + j) * 2 + half
                    if n == 0:
                        pe.wait_ge(m_rows, it * 64 + 64)
                    if not known(it) or it * NS + n >= 3:
                        pe.wait_ge(s_read, it * NS + (n - 2))
                    for a, b, kb, var in score_cols(T):
                        if a // GW == half:
                            last = nc.tensor.matmul(ring[n % 3][:, a - half * GW:b - half * GW],
                                                    KP[s][:, var, j, kb * P:(kb + 1) * P], QP[s][:, var, j, a:b],
                                                    start=True, stop=True)
                    last.then_inc(s_filled, 1)

                def weigh(it, T, s, quarter):
                    if quarter == 0:
                        pe.wait_ge(masked, it * (NT * HQ) + (T + 1) * HQ)
                        if T == 0:
                            pe.wait_ge(m_read, it * MS + MS)
                            if not known(it) or it > 0:
                                pe.wait_ge(out_read, it)
                    q0, q1 = quarter * (GW // 2), (quarter + 1) * (GW // 2)
                    for a, b, kb, var in score_cols(T):
                        a, b = max(a, q0), min(b, q1)
                        if a < b:
                            for j in range(HQ):
                                last = nc.tensor.matmul(OUT[j * HP:(j + 1) * HP, a:b],
                                                        V[s][:, kb * P + j * HP:kb * P + (j + 1) * HP],
                                                        PR[T % 3][:, j, a:b], start=(T == 0 and a % GW == 0),
                                                        stop=(T == NT - 1), skip_group_check=True)
                    if quarter == 3:
                        last.then_inc(pv_done, 1)

                def pair(it, s, last_pair, loads=None):
                    s1, s2 = (s + 1) % SLOTS1, (s + 2) % SLOTS1
                    issued, early = EARLY, 0
                    maxima = (NT - LAG - 1) * HQ * 2
                    for T in range(NT):
                        for j in range(HQ):
                            for half in range(2):
                                if T + LAG < NT:
                                    scores(it, T + LAG, j, half, s)
                                elif not last_pair:
                                    scores(it + 1, T + LAG - NT, j, half, s1)
                                if last_pair:
                                    continue
                                want = EARLY + min(NM - EARLY, -(-(NM - EARLY) * ((T * HQ + j) * 2 + half + 1) // maxima))
                                while issued < want:
                                    max_scores(it + 1, issued, s1)
                                    issued += 1
                                if T < NT - LAG:
                                    continue
                                if early == 0:
                                    pe.wait_ge(pack_loaded[s2], loads)
                                want = -(-EARLY * (((T - NT + LAG) * HQ + j) * 2 + half + 1) // (LAG * HQ * 2))
                                while early < want:
                                    max_scores(it + 2, early, s2)
                                    early += 1
                            if T == NT - LAG - 1 and not last_pair:
                                if j < 2:
                                    turn_max(it + 1, NM + j, s1)
                                else:
                                    values(it + 1, NM + j, s1)
                            for quarter in {0: (), 1: (), 2: (0, 1), 3: (2, 3)}[j] if T == 0 else (j,):
                                weigh(it, T, s, quarter)

                def packs(it_count, s):
                    pe.wait_ge(pack_loaded[s], it_count)

                pe.wait_ge(cor_loaded, 32)
                packs(LOADS, 0)
                for i in range(NM):
                    max_scores(0, i, 0)
                turn_max(0, NM, 0)
                turn_max(0, NM + 1, 0)
                values(0, NM + 2, 0)
                values(0, NM + 3, 0)
                for T in range(LAG):
                    for j in range(HQ):
                        for half in range(2):
                            scores(0, T, j, half, 0)
                packs(LOADS, 1)
                for i in range(EARLY):
                    max_scores(1, i, 1)
                pair(0, 0, False, LOADS)
                with pe.Fori(0, 2) as k:
                    for r in range(SLOTS1):
                        pair(k * 3 + (r + 1), (r + 1) % SLOTS1, False, k * LOADS + 2 * LOADS)
                pair(NIT - 1, (NIT - 1) % SLOTS1, True)

            @block.scalar
            def _(act):
                def pair(it):
                    for T in range(NT):
                        for i in range(2 * HQ):
                            n, half = T * HQ * 2 + i, i % 2
                            act.wait_ge(s_filled, it * NS + (n + 1))
                            if i == 0 and not (known(it) and T < 3):
                                act.wait_ge(pv_done, it * NT + (T - 2))
                            nc.scalar.activation(PR[T % 3][:, i // 2, half * GW:(half + 1) * GW], ring[n % 3][:],
                                                 ACT.Exp).then_inc(s_read, 1)
                pair(0)
                with act.Fori(1, NIT) as it:
                    pair(it)

            @block.vector
            def _(dve):
                def take_max(it, i, s):
                    sb_, j, half = i // (2 * HQ), (i // 2) % HQ, i % 2
                    dve.wait_ge(m_filled, it * MS + (i + 1))
                    out = half_max[:, j, sb_, half:half + 1]
                    if sb_ // 4 == half:
                        c = 384 - (sb_ % 4) * P
                        dve.nop(nofuse=True)
                        nc.vector.tensor_tensor_reduce(out=junk[:, j % 2, :], in0=mring[(s * MS + i) % 3][:], in1=COR[:, c:c + GW], scale=1.0,
                                                       scalar=-3.0e38, op0=ALU.mult, op1=ALU.max, accum_out=out).then_inc(m_read, 1)
                    else:
                        nc.vector.tensor_reduce(out, mring[(s * MS + i) % 3][:], AX.X, ALU.max).then_inc(m_read, 1)

                def finish_max(it, s):
                    dve.wait_ge(m_read, it * MS + NM)
                    hm = half_max[:].rearrange("p j b a -> p (j b) a")
                    nc.vector.tensor_reduce(neg[:], hm, AX.X, ALU.max).then_inc(neg_done, 1)
                    dve.wait_ge(neg_done, it * 4 + 1)
                    nc.vector.tensor_scalar(neg[:], neg[:], -1.0, None, ALU.mult).then_inc(neg_done, 1)
                    dve.wait_ge(neg_done, it * 4 + 2)
                    nc.vector.tensor_copy(neg_part[:, 0, :], neg[:]).then_inc(neg_done, 1)
                    dve.wait_ge(neg_done, it * 4 + 3)
                    nc.vector.tensor_tensor(neg_part[:, 1, :], neg[:], neg_part[:, 0, :], ALU.subtract).then_inc(neg_done, 1)
                    if not known(it) or it > 0:
                        dve.wait_ge(m_rows, it * 64)
                    for part in range(2):
                        i = NM + part
                        dve.wait_ge(m_filled, it * MS + (i + 1))
                        nc.vector.tensor_copy(MT[:, part, :], mring[(s * MS + i) % 3][0:HQ * KB, 0:P // 2].bitcast(BF16)).then_inc(m_read, 1)
                    if not known(it) or it > 2:
                        dve.wait_ge(pv_done, (it - 2) * NT)
                    for half in range(2):
                        i = NM + 2 + half
                        dve.wait_ge(m_filled, it * MS + (i + 1))
                        heads = V[s][:].rearrange("p (n c) -> p n c", c=HP)[:, half * 16:half * 16 + 16, 0:HD]
                        src = mring[(s * MS + i) % 3][:].rearrange("p (n c) -> p n c", c=HP)[:, :, 0:HD]
                        nc.vector.tensor_copy(heads, src).then_inc(m_read, 1)

                def copy_out(it):
                    dve.wait_ge(pv_done, it * NT + NT)
                    if not known(it) or it > 0:
                        dve.wait_ge(out_stored, it * 16)
                    nc.vector.tensor_copy(OST[:], OUT[:]).then_inc(out_read, 1)

                def pair(it, s, first, last_pair):
                    for i in range(EARLY, NM):
                        if i == EARLY + 2 and not first:
                            copy_out(it - 1)
                        if not last_pair:
                            take_max(it + 1, i, (s + 1) % SLOTS1)
                    if not last_pair:
                        finish_max(it + 1, (s + 1) % SLOTS1)
                        for i in range(EARLY):
                            take_max(it + 2, i, (s + 2) % SLOTS1)

                set_slot(dve, nc.vector, 0)
                for s in range(SLOTS1):
                    nc.vector.memset(V[s][:], 0.0).then_inc(v_set, 1)
                dve.wait_ge(v_set, SLOTS1)
                for s in range(SLOTS1):
                    ones = V[s][:].rearrange("p (n c) -> p n c", c=HP)[:, :, HD:HD + 1]
                    nc.vector.memset(ones, 1.0).then_inc(v_set, 1)
                dve.wait_ge(v_set, 2 * SLOTS1)
                set_slot(dve, nc.vector, 2)
                dve.wait_ge(cor_loaded, 32)
                for i in range(NM):
                    take_max(0, i, 0)
                finish_max(0, 0)
                for i in range(EARLY):
                    take_max(1, i, 1)
                pair(0, 0, True, False)
                with dve.Fori(0, 2) as k:
                    for r in range(SLOTS1):
                        pair(k * 3 + (r + 1), (r + 1) % SLOTS1, False, False)
                pair(NIT - 1, (NIT - 1) % SLOTS1, False, True)
                copy_out(NIT - 1)


def normalise(nc, OD, OALL, row_of):
    NR = NIT * HQ
    with ExitStack() as ctx:
        sb, pb, sem = sbuf(nc, ctx), psum(nc, ctx), Sems(nc, ctx)
        pick = sb("n_pick", [NR, NIT, P], F32)
        sums, rec = sb("n_sums", [NR, S], F32), sb("n_rec", [NR, S], F32)
        psB = [pb(f"n_psB{r}") for r in range(4)]
        sums_loaded, pick_loaded, inverse, spread, scaled = (
            sem(f"n_{n}") for n in ("sums_loaded", "pick_loaded", "inverse", "spread", "scaled"))
        loaded = [sem(f"n_loaded{it}") for it in range(NIT)]
        steps = [(it, half) for half in range(2) for it in range(NIT)]
        with nc.Block() as block:
            @block.sync
            def _(sp):
                heads = OD.rearrange("a (j d) s -> (a j) d s", d=HP)
                sp.dma_start(sums[:], heads[:, HD, :]).then_inc(sums_loaded, 16)
                sp.dma_start(pick[:], row_of).then_inc(pick_loaded, 16)
                for it in range(NIT):
                    sp.dma_start(OALL[:, it, :], OD[it]).then_inc(loaded[it], 16)

            @block.tensor
            def _(pe):
                pe.wait_ge(pick_loaded, 16)
                for u, (it, half) in enumerate(steps):
                    pe.wait_ge(inverse, half + 1)
                    if u >= 4:
                        pe.wait_ge(scaled, u - 3)
                    nc.tensor.matmul(psB[u % 4][:], pick[:, it, :], rec[:, half * GW:(half + 1) * GW],
                                     start=True, stop=True).then_inc(spread, 1)

            @block.vector
            def _(dve):
                dve.wait_ge(sums_loaded, 16)
                for half in range(2):
                    cols = slice(half * GW, (half + 1) * GW)
                    nc.vector.reciprocal(rec[:, cols], sums[:, cols]).then_inc(inverse, 1)
                for u, (it, half) in enumerate(steps):
                    dve.wait_ge(loaded[it], 16)
                    dve.wait_ge(spread, u + 1)
                    o = OALL[:, it, half * GW:(half + 1) * GW]
                    nc.vector.tensor_tensor(o, o, psB[u % 4][:], ALU.mult).then_inc(scaled, 1)
                dve.wait_ge(scaled, 2 * NIT)


G1 = 32


def route_l1(nc, X, wr, earlier, consts, GT):
    with ExitStack() as ctx:
        sb, pb, sem = sbuf(nc, ctx), psum(nc, ctx), Sems(nc, ctx)
        W = sb("r1_W", [P, NE1], F32)
        tri = sb("r1_tri", [P, NE1, NE1], F32)
        lg, pr = sb("r1_lg", [P, NT_TOK, NE1], F32), sb("r1_pr", [P, NT_TOK, NE1], F32)
        sm = sb("r1_sm", [P, NT_TOK], F32)
        t1, t2 = (sb(f"r1_{n}", [P, NT_TOK, NE1, NE1], F32) for n in ("t1", "t2"))
        gates = sb("r1_gates", [P, NT_TOK, 2, G1], F32)
        psL = pb("r1_psL")
        psT = [pb(f"r1_psT{g}") for g in range(NG)]
        loaded, logits, shifted, exped, step, copied, turned = (
            sem(f"r1_{n}") for n in ("loaded", "logits", "shifted", "exped", "step", "copied", "turned"))
        with nc.Block() as block:
            @block.sync
            def _(sp):
                sp.dma_start(W[:], wr).then_inc(loaded, 16)
                sp.dma_start(tri[:], earlier.partition_broadcast(P)).then_inc(loaded, 16)

            @block.tensor
            def _(pe):
                pe.wait_ge(loaded, 32)
                for t in range(NT_TOK):
                    last = nc.tensor.matmul(psL[:, t * NE1:(t + 1) * NE1], X[:, t * P:(t + 1) * P], W[:], start=True, stop=True)
                last.then_inc(logits, 1)
                pe.wait_ge(copied, 2)
                for t in range(NT_TOK):
                    last = nc.tensor.transpose(psT[t // 4][0:2 * G1, (t % 4) * P:(t % 4 + 1) * P],
                                               gates[:, t].rearrange("p a e -> p (a e)"), consts["ident"][:])
                    if t % 4 == 3:
                        last.then_inc(turned, 1)

            @block.scalar
            def _(act):
                act.wait_ge(shifted, 1)
                nc.scalar.activation(pr[:], lg[:], ACT.Exp).then_inc(exped, 1)

            @block.vector
            def _(dve):
                n = [0]

                def link(ins):
                    n[0] += 1
                    ins.then_inc(step, 1)
                    dve.wait_ge(step, n[0])

                v = nc.vector
                wide = lambda t: t.unsqueeze(2).to_broadcast([P, NT_TOK, NE1])
                link(v.memset(gates[:], 0.0))
                for a in range(2):
                    link(v.memset(gates[:, :, a, NE1:NE1 + 1], 1.0))
                dve.wait_ge(loaded, 32)
                dve.wait_ge(logits, 1)
                psl = psL[:, 0:NT_TOK * NE1].rearrange("p (t e) -> p t e", e=NE1)
                link(v.tensor_reduce(sm[:], psl, AX.X, ALU.max))
                v.tensor_tensor(lg[:], psl, wide(sm[:]), ALU.subtract).then_inc(shifted, 1)
                dve.wait_ge(exped, 1)
                link(v.tensor_reduce(sm[:], pr[:], AX.X, ALU.add))
                link(v.reciprocal(sm[:], sm[:]))
                link(v.tensor_tensor(pr[:], pr[:], wide(sm[:]), ALU.mult))
                other = pr[:].unsqueeze(2).to_broadcast([P, NT_TOK, NE1, NE1])
                own = pr[:].unsqueeze(3).to_broadcast([P, NT_TOK, NE1, NE1])
                link(v.tensor_tensor(t1[:], other, own, ALU.is_gt))
                link(v.tensor_tensor(t2[:], other, own, ALU.is_equal))
                link(v.tensor_tensor(t2[:], t2[:], tri[:].unsqueeze(1).to_broadcast([P, NT_TOK, NE1, NE1]), ALU.mult))
                link(v.tensor_tensor(t1[:], t1[:], t2[:], ALU.add))
                link(v.tensor_reduce(lg[:], t1[:], AX.X, ALU.add))
                link(v.tensor_scalar(lg[:], lg[:], 2.0, None, ALU.is_lt))
                link(v.tensor_tensor(pr[:], pr[:], lg[:], ALU.mult))
                link(v.tensor_reduce(sm[:], pr[:], AX.X, ALU.add))
                link(v.reciprocal(sm[:], sm[:]))
                for a in range(2):
                    v.tensor_tensor(gates[:, :, a, 0:NE1], pr[:], wide(sm[:]), ALU.mult).then_inc(copied, 1)
                for g in range(NG):
                    dve.wait_ge(turned, g + 1)
                    cols = slice(g * GW, (g + 1) * GW)
                    link(v.tensor_copy(GT[:, cols], psT[g][0:2 * G1, :]))
                    link(v.tensor_tensor(GT[G1:2 * G1, cols], psT[g][G1:2 * G1, :], GT[G1:2 * G1, cols].bitcast(F32), ALU.subtract))


def experts_l1(nc, X, Y, GT, w_experts, sel_experts, bias_fc, bias_proj):
    NX = NE1 + 1
    SE = NG * CH1
    with ExitStack() as ctx:
        sb, pb, sem = sbuf(nc, ctx), psum(nc, ctx), Sems(nc, ctx)
        XH, XL = sb("e1_XH", [P, TOK], F32R), sb("e1_XL", [P, TOK], F32R)
        RAW = [sb(f"e1_RAW{s}", [P, 2, HID], F32) for s in range(2)]
        WH = [sb(f"e1_WH{s}", [P, 2, HID], F32R) for s in range(2)]
        WL = [sb(f"e1_WL{s}", [P, 2, HID], F32R) for s in range(2)]
        SELF = [sb(f"e1_SELF{s}", [2 * G1, P], F32) for s in range(2)]
        SEL = [sb(f"e1_SEL{s}", [2 * G1, P], F32R) for s in range(2)]
        BF = sb("e1_BF", [P, NX * CH1], F32)
        BP = sb("e1_BP", [2 * G1, P], F32)
        GL = [sb(f"e1_GL{s}", [P, GW], F32) for s in range(2)]
        HT = [sb(f"e1_H{s}", [P, GW], F32) for s in range(4)]
        HH = [sb(f"e1_HH{s}", [P, GW], F32R) for s in range(4)]
        HL = [sb(f"e1_HL{s}", [P, GW], F32R) for s in range(4)]
        LAG = 3
        acc = [pb(f"e1_acc{g}") for g in range(NG)]
        psF = [pb(f"e1_psF{s}") for s in range(2)]
        psR = [pb(f"e1_psR{s}") for s in range(2)]
        x_split, bias_loaded = sem("x_split"), sem("bias_loaded")
        w_loaded = [sem(f"w_loaded{s}") for s in range(2)]
        w_split = [sem(f"w_split{s}") for s in range(2)]
        hid_ready, gate_ready, gelu_done, h_ready, high_done, low_done, down_done, y_done = (
            sem(n) for n in ("hid_ready", "gate_ready", "gelu_done", "h_ready", "high_done", "low_done", "down_done", "y_done"))
        with nc.Block() as block:
            @block.sync
            def _(sp):
                def load(e, s):
                    sp.dma_start(RAW[s][:], w_experts[bass.ds(e, 1)].rearrange("a p k n -> (a p) k n")).then_inc(w_loaded[s], 16)
                    sp.dma_start(SELF[s][:], sel_experts[bass.ds(e, 1)].rearrange("a p n -> (a p) n")).then_inc(w_loaded[s], 16)
                load(0, 0)
                sp.dma_start(BF[:], bias_fc).then_inc(bias_loaded, 16)
                sp.dma_start(BP[:], bias_proj).then_inc(bias_loaded, 16)
                load(1, 1)
                with sp.Fori(1, NX // 2) as k:
                    for s in range(2):
                        sp.wait_ge(w_split[s], k * 3)
                        sp.nop(nofuse=True)
                        load(k * 2 + s, s)
                sp.wait_ge(w_split[0], NX // 2 * 3)
                load(NX - 1, 0)

            @block.gpsimd
            def _(pool):
                def split(count, s):
                    pool.wait_ge(w_loaded[s], count * 32 + 32)
                    if not isinstance(count, int) or count:
                        pool.wait_ge(down_done, (count * 2 + (s - 1)) * SE)
                    pool.nop(nofuse=True)
                    nc.gpsimd.tensor_copy(WH[s][:], RAW[s][:]).then_inc(w_split[s], 1)
                    nc.gpsimd.tensor_copy(SEL[s][:], SELF[s][:]).then_inc(w_split[s], 1)
                    pool.wait_ge(w_split[s], count * 3 + 2)
                    nc.gpsimd.tensor_tensor(WL[s][:], RAW[s][:], WH[s][:].bitcast(F32), ALU.subtract).then_inc(w_split[s], 1)
                split(0, 0)
                split(0, 1)
                with pool.Fori(1, NX // 2) as k:
                    split(k, 0)
                    split(k, 1)
                split(NX // 2, 0)

            @block.tensor
            def _(pe):
                def down(n, s, i):
                    g, c = i // CH1, i % CH1
                    pe.wait_ge(low_done, n + 1)
                    for w, h in ((WH, HH), (WL, HH), (WH, HL)):
                        last = nc.tensor.matmul(acc[g][:], w[s][:, 1, c * P:(c + 1) * P], h[i % 4][:], start=False, stop=True,
                                                skip_group_check=True)
                    last.then_inc(down_done, 1)

                def expert(e, count, s):
                    peeled = isinstance(e, int)
                    pe.wait_ge(w_split[s], count * 3 + 3)
                    for i in range(SE):
                        n = e * SE + i
                        g, c = i // CH1, i % CH1
                        cols = slice(g * GW, (g + 1) * GW)
                        if c == 0:
                            if not (peeled and i < 2 * CH1):
                                pe.wait_ge(h_ready, e * SE + (i - CH1))
                            nc.tensor.matmul(psR[g % 2][:], SEL[s][:], GT[:, cols], start=True, stop=True).then_inc(gate_ready, 1)
                        if not (peeled and i < 2):
                            pe.wait_ge(gelu_done, n - 1)
                        nc.tensor.matmul(psF[i % 2][:], WH[s][:, 0, c * P:(c + 1) * P], XH[:, cols], start=True, stop=False)
                        nc.tensor.matmul(psF[i % 2][:], WH[s][:, 0, c * P:(c + 1) * P], XL[:, cols], start=False, stop=False)
                        nc.tensor.matmul(psF[i % 2][:], WL[s][:, 0, c * P:(c + 1) * P], XH[:, cols], start=False, stop=True)\
                            .then_inc(hid_ready, 1)
                        if not (peeled and e == 0 and i < LAG):
                            down(n - LAG, s if i >= LAG else 1 - s, (i - LAG) % SE)

                pe.wait_ge(bias_loaded, 32)
                for g in range(NG):
                    nc.tensor.matmul(acc[g][:], BP[:], GT[:, g * GW:(g + 1) * GW].bitcast(F32), start=True, stop=True)
                pe.wait_ge(x_split, 2)
                expert(0, 0, 0)
                with pe.Fori(0, NX // 2) as k:
                    expert(k * 2 + 1, k, 1)
                    expert(k * 2 + 2, k + 1, 0)
                for i in range(SE - LAG, SE):
                    down((NX - 1) * SE + i, 0, i)

            @block.scalar
            def _(act):
                act.wait_ge(bias_loaded, 32)

                def gelu(e, i, free):
                    n = e * SE + i
                    act.wait_ge(hid_ready, n + 1)
                    if free:
                        act.wait_ge(h_ready, n - 1)
                    act.nop(nofuse=True)
                    nc.scalar.activation(GL[i % 2][:], psF[i % 2][:], ACT.Gelu_apprx_tanh,
                                         bias=BF[:, bass.ds(e * CH1 + i % CH1, 1)]).then_inc(gelu_done, 1)

                def high(n, i, free):
                    act.wait_ge(h_ready, n + 1)
                    if free:
                        act.wait_ge(down_done, n - 3)
                    nc.scalar.activation(HH[i % 4][:], HT[i % 4][:], ACT.Copy).then_inc(high_done, 1)

                for i in range(SE):
                    gelu(0, i, i >= 2)
                    if i:
                        high(i - 1, i - 1, i - 1 >= 4)
                with act.Fori(1, NX) as e:
                    for i in range(SE):
                        gelu(e, i, True)
                        high(e * SE + (i - 1), (i - 1) % SE, True)
                high(NX * SE - 1, SE - 1, True)

            @block.vector
            def _(dve):
                nc.vector.tensor_copy(XH[:], X[:]).then_inc(x_split, 1)
                dve.wait_ge(x_split, 1)
                nc.vector.tensor_tensor(XL[:], X[:], XH[:].bitcast(F32), ALU.subtract).then_inc(x_split, 1)

                def low(n, i):
                    dve.wait_ge(high_done, n + 1)
                    nc.vector.tensor_tensor(HL[i % 4][:], HT[i % 4][:], HH[i % 4][:].bitcast(F32), ALU.subtract).then_inc(low_done, 1)

                def hidden(e, i):
                    n = e * SE + i
                    if not (isinstance(e, int) and i < 4):
                        dve.wait_ge(low_done, n - 3)
                    if i % CH1 == 0:
                        dve.wait_ge(gate_ready, e * NG + (i // CH1 + 1))
                    dve.wait_ge(gelu_done, n + 1)
                    nc.vector.tensor_tensor(HT[i % 4][:], GL[i % 2][:], psR[(i // CH1) % 2][:], ALU.mult).then_inc(h_ready, 1)
                for i in range(SE):
                    hidden(0, i)
                    if i:
                        low(i - 1, i - 1)
                with dve.Fori(1, NX) as e:
                    for i in range(SE):
                        hidden(e, i)
                        low(e * SE + (i - 1), (i - 1) % SE)
                low(NX * SE - 1, SE - 1)
                dve.wait_ge(down_done, NX * SE)
                for g in range(NG):
                    cols = slice(g * GW, (g + 1) * GW)
                    nc.vector.tensor_tensor(Y[:, cols], X[:, cols], acc[g][:], ALU.add).then_inc(y_done, 1)
                dve.wait_ge(y_done, NG)


def build(nc, a, out):
    q0 = nc.dram_tensor("q0_parts", (H, NPART, HD, TOK), BF16).ap()
    k0 = nc.dram_tensor("k0_parts", (H, NPART + 2, HD, TOK), BF16).ap()
    qn0 = nc.dram_tensor("q0_norm_parts", (H, NPART, TOK), BF16).ap()
    kn0 = nc.dram_tensor("k0_norm_parts", (H, NPART, TOK), BF16).ap()
    q1 = nc.dram_tensor("q1_parts", (2, H, NPART, HD, TOK), BF16).ap()
    k1 = nc.dram_tensor("k1_parts", (2, H, NPART + 2, HD, TOK), BF16).ap()
    lat = nc.dram_tensor("latent", (DL, TOK), F32).ap()
    o1 = nc.dram_tensor("o1_sums", (NIT, P, S), F32).ap()
    with ExitStack() as ctx:
        sb = sbuf(nc, ctx)
        X = sb("X", [P, TOK], F32)
        mean_of, ident = sb("mean_of", [P, P], F32), sb("ident", [P, P], F32)
        eps = sb("eps", [P, 1], F32)
        consts = dict(mean_of=mean_of, ident=ident, eps=eps)
        loaded = Sems(nc, ctx)("x_loaded")
        with nc.Block() as block:
            @block.sync
            def _(sp):
                for tile, src in ((X, a["xT"]), (mean_of, a["mean_of"]), (ident, a["ident"]), (eps, a["eps"])):
                    sp.dma_start(tile[:], src).then_inc(loaded, 16)
                sp.wait_ge(loaded, 64)

        def output_terms(quads, OALL):
            def terms(g):
                b, half = g // 2, g % 2
                return [(quads[:, q, :], OALL[:, b * NQUAD + q, half * GW:(half + 1) * GW]) for q in range(NQUAD)]
            return terms

        project_l0(nc, X, a["wq0"], a["wk0"], a["head_sum"], q0, k0, qn0, kn0)
        with ExitStack() as part:
            OALL = sbuf(nc, part)("OALL0", [P, NIT, S], F32)
            attention_l0(nc, a["xT"], a["wv0"], a["gamma"], q0, k0, qn0, kn0, OALL)
            Y, WO = sbuf(nc, part)("Y_a0", [P, TOK], F32), sbuf(nc, part)("WO0", [P, NQUAD, P], F32)
            add_and_norm(nc, "n0a", X, Y, consts, output_terms(WO, OALL), ((WO[:], a["wo0"].rearrange("q p n -> p q n")),))
        with ExitStack() as part:
            Y, GT = sbuf(nc, part)("Y_m0", [P, TOK], F32), sbuf(nc, part)("GT0", [P, TOK], F32R)
            route_l0(nc, X, a["gate_w"], a["gate_bias"], a["earlier"], consts, GT)
            experts_l0(nc, X, Y, GT, a["w_chunks"], a["sel_chunks"])
            add_and_norm(nc, "n0m", X, Y, consts)
        project_l1(nc, X, {n: a[n] for n in ("wq", "wk", "wv", "down", "upk")}, a["decays"], q1, k1, lat)
        attention_l1(nc, a["upv"], a["correct"], a["ident16"], q1, k1, lat, o1)
        with ExitStack() as part:
            OALL = sbuf(nc, part)("OALL1", [P, NIT, S], F32)
            normalise(nc, o1, OALL, a["den_rows"])
            Y, WO = sbuf(nc, part)("Y_a1", [P, TOK], F32), sbuf(nc, part)("WO1", [P, NQUAD, P], F32)
            add_and_norm(nc, "n1a", X, Y, consts, output_terms(WO, OALL), ((WO[:], a["wo1"].rearrange("q p n -> p q n")),))
        with ExitStack() as part:
            Y, GT = sbuf(nc, part)("Y_m1", [P, TOK], F32), sbuf(nc, part)("GT1", [2 * G1, TOK], F32R)
            route_l1(nc, X, a["wr"], a["earlier"], consts, GT)
            experts_l1(nc, X, Y, GT, a["w_experts"], a["sel_experts"], a["bias_fc"], a["bias_proj"])
            add_and_norm(nc, "n1m", X, Y, consts, out=out)


def kernel(**inputs):
    import concourse.bacc as bacc
    import ml_dtypes
    from concourse.bass_utils import run_bass_kernel_spmd

    w = {n: np.asarray(v) for n, v in inputs.items()}

    def by_quad(m):
        o = np.zeros((NQUAD, m.shape[0], HQ, HP), m.dtype)
        o[..., :HD] = m.reshape(m.shape[0], NQUAD, HQ, HD).transpose(1, 0, 2, 3)
        return o.reshape(NQUAD, m.shape[0], P)

    def stacked(routed, shared):
        o = np.zeros((CHS + CH0, P, P), routed.dtype)
        o.reshape(-1, P)[:SHI] = shared
        o.reshape(-1, P)[CHS * P:] = routed.reshape(-1, P)
        return o

    gate = stacked(w["L0_ffn_Wg"], w["L0_ffn_Sg"]).transpose(0, 2, 1)
    up = stacked(w["L0_ffn_Wu"], w["L0_ffn_Su"]).transpose(0, 2, 1)
    down = stacked(w["L0_ffn_Wd"].transpose(0, 2, 1), w["L0_ffn_Sd"].T)
    sel0 = np.zeros((CHS + CH0, 2, NE0, P), np.float32)
    rows = np.arange(CH0 * P)
    sel0[CHS + rows // P, :, rows // I0, rows % P] = 1
    first = np.concatenate([w["L1_ffn_Wfc"], w["L1_ffn_Wfc_s"][None]])
    second = np.concatenate([w["L1_ffn_Wproj"], w["L1_ffn_Wproj_s"][None]])
    second = second.reshape(NE1 + 1, CH1, P, P).transpose(0, 2, 1, 3).reshape(NE1 + 1, P, HID)
    bias_fc = np.concatenate([w["L1_ffn_bfc"], w["L1_ffn_bfc_s"][None]]).reshape(-1, P).T
    bias_proj = np.zeros((2, G1, P), np.float32)
    bias_proj[:, :NE1 + 1] = np.concatenate([w["L1_ffn_bproj"], w["L1_ffn_bproj_s"][None]])
    sel1 = np.zeros((NE1 + 1, 2, G1, P), np.float32)
    for e in range(NE1 + 1):
        sel1[e, :, e] = 1
    pos = DECAY * (np.arange(S) - S // 2)
    scale = E ** -0.5
    decays = np.stack([scale * np.exp(pos), scale * np.exp(-pos), np.exp(-pos), np.exp(pos)])
    correct = np.ones((P, 896))
    row, col = np.arange(P)[:, None], np.arange(P)[None, :]
    correct[:, 384:512] = np.exp(-2 * DECAY * np.maximum(col - row, 0))
    den_rows = np.repeat(np.eye(NIT * HQ), HP, 1).astype(np.float32)
    arrays = {
        "xT": w["L0_attn_q"].reshape(TOK, E).T,
        "wq0": w["L0_attn_Wq"], "wk0": w["L0_attn_Wk"], "wv0": by_quad(w["L0_attn_Wv"]),
        "wo0": by_quad(w["L0_attn_Wo"].T).transpose(0, 2, 1), "gamma": w["L0_attn_gamma"],
        "head_sum": np.repeat(np.eye(H, 32), HD, 0).astype(np.float32),
        "gate_w": w["L0_ffn_gate_w"].T, "gate_bias": w["L0_ffn_gate_bias"],
        "earlier": np.tril(np.ones((NGRP, NGRP)), -1).astype(np.float32),
        "w_chunks": np.stack([gate, up, down], 2), "sel_chunks": sel0.reshape(-1, P, P),
        "wq": w["L1_attn_W_q"], "wk": w["L1_attn_W_k"], "wv": w["L1_attn_W_v"], "down": w["L1_attn_W_down_kv"],
        "upk": w["L1_attn_W_up_k"], "upv": by_quad(w["L1_attn_W_up_v"]),
        "wo1": by_quad(w["L1_attn_W_o"].T).transpose(0, 2, 1), "decays": decays.astype(np.float32),
        "correct": correct.astype(np.float32), "ident16": np.eye(P).astype(ml_dtypes.bfloat16),
        "ident": np.eye(P).astype(np.float32), "mean_of": np.full((P, P), 1 / E, np.float32),
        "eps": np.full((P, 1), EPS, np.float32), "den_rows": den_rows.reshape(NIT * HQ, NIT, P), "wr": w["L1_ffn_Wr"],
        "w_experts": np.stack([first, second], 2), "sel_experts": sel1.reshape(NE1 + 1, 2 * G1, P),
        "bias_fc": bias_fc, "bias_proj": bias_proj.reshape(2 * G1, P),
    }
    arrays = {f"in_{n}": np.ascontiguousarray(v) for n, v in arrays.items()}
    nc = bacc.Bacc("TRN2", target_bir_lowering=False, num_devices=1)
    aps = {n[3:]: nc.dram_tensor(n, v.shape, mybir.dt.from_np(v.dtype), kind="ExternalInput").ap() for n, v in arrays.items()}
    out = nc.dram_tensor("out_xT", (P, TOK), F32, kind="ExternalOutput").ap()
    build(nc, aps, out)
    r = run_bass_kernel_spmd(nc, [arrays], core_ids=[0])
    return r.results[0]["out_xT"].T.reshape(B, S, E)
```
